# Optimizing a Trainium2 kernel written in Bass

```python
import numpy as np
import jax
import jax.numpy as jnp

def _softmax(x, axis=-1):
    return jax.nn.softmax(x, axis=axis)

def _gelu(x):
    return jax.nn.gelu(x, approximate=True)

def _silu(x):
    return jax.nn.silu(x)

def _sigmoid(x):
    return jax.nn.sigmoid(x)

def _layernorm(x, axis=-1, eps=1e-05):
    m = jnp.mean(x, axis=axis, keepdims=True)
    v = jnp.var(x, axis=axis, keepdims=True)
    return (x - m) / jnp.sqrt(v + eps)

def _scatter_add(tgt, idx, src, axis=0):
    return tgt.at[idx].add(src)

def _segment_sum(src, seg, n):
    return jax.ops.segment_sum(src, seg, n)
kernel_name = 'mk_vit_tower_d1_tok_img768_r4_614731'

def setup_inputs(seed: int=0):
    np.random.seed(seed)
    _w = jnp.asarray

    def _rec_inputs():
        import jax
        import jax.numpy as jnp
        _rk = jax.random.key(seed)
        x = -0.000356955 + 1 * jax.random.normal(jax.random.fold_in(_rk, 1), (128, 3, 224, 224), jnp.float32)
        return x
    x = _rec_inputs()

    def _L0_tok_setup():
        import jax, jax.numpy as jnp
        import numpy as np
        P = 16
        PW = P // 2 + 1
        key = jax.random.key(seed)
        ks = jax.random.split(key, 5)
        B, C, H, W = (128, 3, 224, 224)
        E = 192
        N = H // P * (W // P)
        return {'x': jax.random.normal(ks[0], (B, C, H, W), dtype=jnp.float32), 'freq_weight_h': jnp.ones((P,), dtype=jnp.float32), 'freq_weight_w': jnp.ones((PW,), dtype=jnp.float32), 'proj_w': jax.random.normal(ks[1], (E, C * P * PW), dtype=jnp.float32) * 0.02, 'proj_b': jnp.zeros((E,), dtype=jnp.float32), 'cls_token': jax.random.normal(ks[2], (1, 1, E), dtype=jnp.float32), 'pos_emb': jax.random.normal(ks[3], (1, N + 1, E), dtype=jnp.float32)}
    _L0_tok_all = _L0_tok_setup()
    _L0_tok_in = {k: v for k, v in _L0_tok_all.items() if k in ('freq_weight_h', 'freq_weight_w', 'proj_w', 'proj_b', 'cls_token', 'pos_emb')}
    del _L0_tok_all

    def _L0_attn_setup():
        import jax, jax.numpy as jnp
        import numpy as np
        B, S, D, H = (64, 577, 192, 12)
        DH = D // H
        key = jax.random.key(seed)
        ks = jax.random.split(key, 9)
        sc = 0.02
        return {'x': jax.random.normal(ks[0], (B, S, D), jnp.float32), 'Wq': jax.random.normal(ks[1], (H, D, DH), jnp.float32) * sc, 'bq': jnp.zeros((H, DH), jnp.float32), 'Wk': jax.random.normal(ks[2], (H, D, DH), jnp.float32) * sc, 'bk': jnp.zeros((H, DH), jnp.float32), 'Wv': jax.random.normal(ks[3], (H, D, DH), jnp.float32) * sc, 'bv': jnp.zeros((H, DH), jnp.float32), 'Wo': jax.random.normal(ks[4], (D, D), jnp.float32) * sc, 'bo': jnp.zeros((D,), jnp.float32)}
    _L0_attn_all = _L0_attn_setup()
    _L0_attn_in = {k: v for k, v in _L0_attn_all.items() if k in ('Wq', 'bq', 'Wk', 'bk', 'Wv', 'bv', 'Wo', 'bo')}
    del _L0_attn_all

    def _L0_ffn_setup():
        import jax, jax.numpy as jnp
        import numpy as np
        DIM = 192
        H = 12
        HD = 64
        SHARED = 2
        ROUTED = 2
        E_ROUTED = H - SHARED
        LN_EPS = 1e-05

        def _layernorm(x, w, b):
            m = x.mean(-1, keepdims=True)
            v = ((x - m) ** 2).mean(-1, keepdims=True)
            return (x - m) * jax.lax.rsqrt(v + LN_EPS) * w + b
        key = jax.random.key(seed)
        ks = jax.random.split(key, 12)
        B, N = (4, 512)
        s = 0.02
        return {'x': jax.random.normal(ks[0], (B, N, DIM), jnp.float32), 'qkv_w': jax.random.normal(ks[1], (DIM, 3 * H * HD), jnp.float32) * s, 'qkv_b': jnp.zeros((3 * H * HD,), jnp.float32), 'q_norm_w': jnp.ones((HD,), jnp.float32), 'q_norm_b': jnp.zeros((HD,), jnp.float32), 'k_norm_w': jnp.ones((HD,), jnp.float32), 'k_norm_b': jnp.zeros((HD,), jnp.float32), 'wg_w': jax.random.normal(ks[2], (DIM, E_ROUTED), jnp.float32) * s, 'wg0_w': jax.random.normal(ks[3], (DIM, 2), jnp.float32) * s, 'wg1_w': jax.random.normal(ks[4], (DIM, SHARED), jnp.float32) * s, 'proj_w': jax.random.normal(ks[5], (H * HD, DIM), jnp.float32) * s, 'proj_b': jnp.zeros((DIM,), jnp.float32)}
    _L0_ffn_all = _L0_ffn_setup()
    _L0_ffn_in = {k: v for k, v in _L0_ffn_all.items() if k in ('qkv_w', 'qkv_b', 'q_norm_w', 'q_norm_b', 'k_norm_w', 'k_norm_b', 'wg_w', 'wg0_w', 'wg1_w', 'proj_w', 'proj_b')}
    del _L0_ffn_all
    return {'x': x, 'L0_tok_freq_weight_h': _L0_tok_in['freq_weight_h'], 'L0_tok_freq_weight_w': _L0_tok_in['freq_weight_w'], 'L0_tok_proj_w': _L0_tok_in['proj_w'], 'L0_tok_proj_b': _L0_tok_in['proj_b'], 'L0_tok_cls_token': _L0_tok_in['cls_token'], 'L0_tok_pos_emb': _L0_tok_in['pos_emb'], 'L0_attn_Wq': _L0_attn_in['Wq'], 'L0_attn_bq': _L0_attn_in['bq'], 'L0_attn_Wk': _L0_attn_in['Wk'], 'L0_attn_bk': _L0_attn_in['bk'], 'L0_attn_Wv': _L0_attn_in['Wv'], 'L0_attn_bv': _L0_attn_in['bv'], 'L0_attn_Wo': _L0_attn_in['Wo'], 'L0_attn_bo': _L0_attn_in['bo'], 'L0_ffn_qkv_w': _L0_ffn_in['qkv_w'], 'L0_ffn_qkv_b': _L0_ffn_in['qkv_b'], 'L0_ffn_q_norm_w': _L0_ffn_in['q_norm_w'], 'L0_ffn_q_norm_b': _L0_ffn_in['q_norm_b'], 'L0_ffn_k_norm_w': _L0_ffn_in['k_norm_w'], 'L0_ffn_k_norm_b': _L0_ffn_in['k_norm_b'], 'L0_ffn_wg_w': _L0_ffn_in['wg_w'], 'L0_ffn_wg0_w': _L0_ffn_in['wg0_w'], 'L0_ffn_wg1_w': _L0_ffn_in['wg1_w'], 'L0_ffn_proj_w': _L0_ffn_in['proj_w'], 'L0_ffn_proj_b': _L0_ffn_in['proj_b']}

def reference(x, L0_tok_freq_weight_h, L0_tok_freq_weight_w, L0_tok_proj_w, L0_tok_proj_b, L0_tok_cls_token, L0_tok_pos_emb, L0_attn_Wq, L0_attn_bq, L0_attn_Wk, L0_attn_bk, L0_attn_Wv, L0_attn_bv, L0_attn_Wo, L0_attn_bo, L0_ffn_qkv_w, L0_ffn_qkv_b, L0_ffn_q_norm_w, L0_ffn_q_norm_b, L0_ffn_k_norm_w, L0_ffn_k_norm_b, L0_ffn_wg_w, L0_ffn_wg0_w, L0_ffn_wg1_w, L0_ffn_proj_w, L0_ffn_proj_b):
    import jax
    import jax.numpy as jnp

    def _L0_tok_ref(x, freq_weight_h, freq_weight_w, proj_w, proj_b, cls_token, pos_emb):
        import jax, jax.numpy as jnp
        import numpy as np
        P = 16
        PW = P // 2 + 1
        B, C, H, W = x.shape
        nH, nW = (H // P, W // P)
        N = nH * nW
        patches = x.reshape(B, C, nH, P, nW, P).transpose(0, 1, 2, 4, 3, 5)
        patches = patches.reshape(B, C, N, P, P)
        x_fft = jnp.fft.rfft2(patches, norm='ortho').real
        x_fft = x_fft * freq_weight_h[None, None, None, :, None]
        x_fft = x_fft * freq_weight_w[None, None, None, None, :]
        x_flat = x_fft.transpose(0, 2, 1, 3, 4).reshape(B, N, C * P * PW)
        x_proj = jnp.einsum('bnf,ef->bne', x_flat, proj_w) + proj_b
        cls = jnp.broadcast_to(cls_token, (B, 1, cls_token.shape[-1]))
        out = jnp.concatenate([cls, x_proj], axis=1) + pos_emb
        return out

    def _L0_attn_ref(x, Wq, bq, Wk, bk, Wv, bv, Wo, bo):
        import jax, jax.numpy as jnp
        import numpy as np
        B, S, D, H = (64, 577, 192, 12)
        DH = D // H
        q = jnp.einsum('bsd,hde->bhse', x, Wq) + bq[None, :, None, :]
        k = jnp.einsum('bsd,hde->bhse', x, Wk) + bk[None, :, None, :]
        v = jnp.einsum('bsd,hde->bhse', x, Wv) + bv[None, :, None, :]
        scale = np.float32(1.0 / np.sqrt(DH))
        scores = jnp.einsum('bhqe,bhke->bhqk', q, k) * scale
        probs = jax.nn.softmax(scores, axis=2)
        ctx = jnp.einsum('bhqk,bhke->bhqe', probs, v)
        ctx = ctx.transpose(0, 2, 1, 3).reshape(x.shape[0], x.shape[1], H * DH)
        return ctx @ Wo + bo

    def _L0_ffn_ref(x, qkv_w, qkv_b, q_norm_w, q_norm_b, k_norm_w, k_norm_b, wg_w, wg0_w, wg1_w, proj_w, proj_b):
        import jax, jax.numpy as jnp
        import numpy as np
        DIM = 192
        H = 12
        HD = 64
        SHARED = 2
        ROUTED = 2
        E_ROUTED = H - SHARED
        LN_EPS = 1e-05

        def _layernorm(x, w, b):
            m = x.mean(-1, keepdims=True)
            v = ((x - m) ** 2).mean(-1, keepdims=True)
            return (x - m) * jax.lax.rsqrt(v + LN_EPS) * w + b
        B, N, C = x.shape
        scale = HD ** (-0.5)
        gates = jax.nn.softmax(x @ wg_w, axis=-1)
        _, idx = jax.lax.top_k(gates, ROUTED)
        mask = jax.nn.one_hot(idx, E_ROUTED, dtype=gates.dtype).sum(-2)
        rg = gates * mask
        denom = jnp.clip(rg.sum(-1, keepdims=True), jnp.finfo(rg.dtype).eps, None)
        routed_gates = rg / denom * ROUTED
        qkv = (x @ qkv_w + qkv_b).reshape(B, N, 3, H, HD)
        qkv = jnp.transpose(qkv, (2, 0, 3, 1, 4))
        q, k, v = (qkv[0], qkv[1], qkv[2])
        q = _layernorm(q, q_norm_w, q_norm_b)
        k = _layernorm(k, k_norm_w, k_norm_b)
        attn = jax.nn.softmax(jnp.einsum('bhqd,bhkd->bhqk', q * scale, k), axis=-1)
        o = jnp.einsum('bhqk,bhkd->bhqd', attn, v)
        o = jnp.transpose(o, (0, 2, 1, 3))
        shared_gates = jax.nn.softmax(x @ wg1_w, axis=-1) * SHARED
        w0 = jax.nn.softmax(x @ wg0_w, axis=-1) * 2.0
        shared_gates = w0[..., 0:1] * shared_gates
        routed_gates = w0[..., 1:2] * routed_gates
        masked_gates = jnp.concatenate([shared_gates, routed_gates], axis=-1)
        o = (masked_gates[..., None] * o).reshape(B, N, H * HD)
        return o @ proj_w + proj_b
    h = _L0_tok_ref(x, L0_tok_freq_weight_h, L0_tok_freq_weight_w, L0_tok_proj_w, L0_tok_proj_b, L0_tok_cls_token, L0_tok_pos_emb)
    h = h + _L0_attn_ref(_layernorm(h, axis=-1), L0_attn_Wq, L0_attn_bq, L0_attn_Wk, L0_attn_bk, L0_attn_Wv, L0_attn_bv, L0_attn_Wo, L0_attn_bo)
    h = h + _L0_ffn_ref(_layernorm(h, axis=-1), L0_ffn_qkv_w, L0_ffn_qkv_b, L0_ffn_q_norm_w, L0_ffn_q_norm_b, L0_ffn_k_norm_w, L0_ffn_k_norm_b, L0_ffn_wg_w, L0_ffn_wg0_w, L0_ffn_wg1_w, L0_ffn_proj_w, L0_ffn_proj_b)
    return h

_drawn_inputs = setup_inputs


def setup_inputs(seed=0):
    import zlib

    import numpy as np

    out = dict(_drawn_inputs(seed))
    spreads = {'L0_tok_freq_weight_h': (1.0, 0.2),
     'L0_tok_freq_weight_w': (1.0, 0.2),
     'L0_tok_proj_b': (0.0, 0.1),
     'L0_attn_bq': (0.0, 0.8),
     'L0_attn_bk': (0.0, 0.8),
     'L0_attn_bv': (0.0, 0.294),
     'L0_attn_bo': (0.0, 0.1),
     'L0_ffn_qkv_b': (0.0, 0.277),
     'L0_ffn_q_norm_w': (1.0, 0.6),
     'L0_ffn_q_norm_b': (0.0, 0.8),
     'L0_ffn_k_norm_w': (1.0, 0.6),
     'L0_ffn_k_norm_b': (0.0, 0.8),
     'L0_ffn_proj_b': (0.0, 0.1)}
    factors = {'L0_attn_Wq': 8.0,
     'L0_attn_Wk': 8.0,
     'L0_attn_Wv': 6.051,
     'L0_ffn_qkv_w': 3.501,
     'L0_ffn_wg_w': 2.834,
     'L0_ffn_wg0_w': 8.0,
     'L0_ffn_wg1_w': 8.0}
    for name, (base, spread) in spreads.items():
        noise = np.random.default_rng([zlib.crc32(name.encode()), seed]).standard_normal(out[name].shape)
        drawn = base * np.exp(spread * noise) if base else spread * noise
        out[name] = jnp.asarray(drawn.astype(out[name].dtype))
    for name, factor in factors.items():
        out[name] = (out[name] * factor).astype(out[name].dtype)
    return out
```

```python
from contextlib import ExitStack

import numpy as np

import concourse.bass as bass
from concourse import mybir

F32 = mybir.dt.float32
I32 = mybir.dt.int32
F16 = mybir.dt.float16
BF16 = mybir.dt.bfloat16
ALU = mybir.AluOpType
ACT = mybir.ActivationFunctionType
AX = mybir.AxisListType

PATCH, SIDE, CH = 16, 14, 3
NPATCH = SIDE * SIDE
PW = PATCH // 2 + 1
T = NPATCH + 1
TC = 99
TP = 2 * TC
D = 192
DK = 96
H = 12
E1 = 16
E2 = 64
KC, KR = 4, 98
LN_EPS = 1e-5
GATE_EPS = float(np.finfo(np.float32).eps)
NG = 14
RSQRT_GUESS = float(0x5F3759DF)
W_SCALE = 256.0
GN_SCALE = 1024.0
PREPARED = 1
GROUP = 4


def fold_pairs():
    first, mirror = [], []
    for h in range(PATCH):
        for w in range(PATCH):
            m = ((-h) % PATCH) * PATCH + (-w) % PATCH
            if h * PATCH + w <= m:
                first.append(h * PATCH + w)
                mirror.append(m)
    return np.array(first), np.array(mirror)


def fold_basis():
    first, mirror = fold_pairs()
    n = len(first)
    u, v = np.divmod(np.arange(PATCH * PW), PW)
    h, w = np.divmod(first, PATCH)
    cos = np.cos(2 * np.pi * ((u[:, None] * h + v[:, None] * w) % PATCH) / PATCH) / PATCH
    cos[:, first == mirror] /= 2
    out = np.zeros((PATCH * PW, CH, KC * KR), np.float32)
    for c in range(CH):
        out[:, c, c * n:(c + 1) * n] = cos
    return np.ascontiguousarray(out.reshape(2, 72, CH, KC * KR).transpose(1, 0, 2, 3))


def shape_constants():
    c = {}
    c["ident"] = np.eye(128, dtype=np.float32)
    sel_var = np.zeros((128, H, 32), np.float32)
    sel_rstd = np.zeros((128, H, 128), np.float32)
    for u in range(H):
        for j in range(2):
            row = 2 * (u // 4) + j
            sel_var[64 * j:64 * j + 64, u, row] = 1.0 / E2
            sel_rstd[32 * (u % 4) + row, u, 64 * j:64 * j + 64] = 1.0
    c["sel_var"], c["sel_rstd"] = sel_var, sel_rstd
    sel_sum = np.zeros((128, 2, H // GROUP, 32), np.float32)
    for ch in range(2):
        for a in range(H // GROUP):
            sel_sum[:TC - ch, ch, a, a] = 1.0
            sel_sum[:TC - ch, ch, a, H // GROUP:] = 1.0
    sel_head = np.zeros((128, H // 2, 128), np.float32)
    for h in range(H):
        sel_head[32 * (h % GROUP) + h // GROUP, h // 2, 64 * (h % 2):64 * (h % 2) + 64] = 1.0 / GN_SCALE
    c["sel_sum"], c["sel_head"] = sel_sum, sel_head
    sel_max = np.zeros((128, GROUP, TC), np.float32)
    for j in range(GROUP):
        sel_max[j, j, :] = -1.0
    c["sel_max"] = sel_max
    mask = np.zeros((DK, 6), np.float32)
    for j in range(6):
        mask[E1 * j:E1 * j + E1, j] = E1 ** -0.5 / W_SCALE
    c["mask1"] = mask
    c["iota"] = np.ascontiguousarray(np.broadcast_to(np.arange(10, dtype=np.float32), (TC, 2, 10)))
    c["center"] = (np.eye(128) - np.kron(np.eye(2), np.ones((64, 64))) / 64).astype(np.float32)
    c["basis"] = fold_basis()
    return c


class Signal:

    def __init__(self, sem, per):
        self.sem, self.per, self.made = sem, per, 0

    def at(self, img, k):
        assert 0 <= k <= self.per
        return self.sem, img * self.per + k

    def up(self, n=1):
        self.made += n
        return self.sem


class Bank:

    def __init__(self, tensor, full, free):
        self.tensor, self.full, self.free = tensor, full, free


BANKS = {"tok": (2,), "x1T": (2,), "q1": (0,), "k1": (1,), "v1": (2,), "s1": (0, 1), "ctx": (2,), "wo": (2,),
         "x2T": (2,), "gl": (5,), "qk": (6, 5), "v2": (6, 5), "var": (7,), "rstd": (3, 4), "gT": (5,),
         "smax": (3, 4), "maxT": (5,), "s2": (3, 4), "o2": (6, 5), "sum": (7,), "gh": (3, 4), "proj": (3, 4)}

ORDER = """
A:fold C:gn B:gl A:tok C:gh0 B:qk0 C:gh1 B:gate0 B:qk1 C:gh2 B:qk2 B:qk3 A:nx1 A:x1T B:qk4 C:gh3 C:gh4 B:qk5 A:q1
B:ms0 A:k1 C:gh5 B:ms1 B:ms2 B:ms3 B:ms4 B:v2_0 B:ms5 A:s1_0 B:var0 A:s1_1 B:var1 B:var2 A:v1 B:var3 B:var4 C:proj
B:v2_1 B:rstd0 A:s1_2 B:v2_2 B:rstd1 A:s1_3 B:smax0 A:s1_4 B:lo0 B:rstd2 B:v2_3 B:h2b B:lo1 B:smax1 B:smax2 A:s1_5
B:rstd3 A:s1_6 B:smax3 B:lo2 B:rstd4 B:rstd5 B:maxT0 A:s1_7 A:ctx0 B:lo3 B:lo4 B:smax4 B:gate1 B:s2_0 A:s1_8 B:smax5
A:s1_9 B:smax6 B:s2_1 B:s2_2 A:s1_10 B:smax7 B:smax8 B:smax9 B:maxT1 B:smax10 A:s1_11 B:o2_0 B:smax11 B:s2_3 B:maxT2
B:s2_4 A:ctx1 B:o2_1 B:s2_5 B:gate2 B:s2_6 A:ctx2 B:lo5 B:gate3 B:s2_7 A:wo B:s2_8 B:s2_9 B:gT B:o2_2 A:nx2 B:sum0
B:s2_10 B:s2_11 A:x2T B:o2_3 B:sum1 B:o2_4 B:o2_5 B:sum2
""".split()


def steps_of(phases):
    for entry in ORDER:
        phase, step = entry.split(":")
        if phase in phases:
            name = step.rstrip("0123456789").rstrip("_")
            if step in ("x1T", "x2T", "q1", "k1", "v1", "nx1", "nx2", "h2b"):
                name = step
            elif step.startswith(("s1_", "s2_", "v2_", "o2_")):
                name = step[:2]
            number = step[len(name):].lstrip("_")
            yield phase, name, int(number) if number else 0


def bank_uses():
    uses, count, turn = {}, [0] * 8, {}
    for _, name, n in [step for phase in "ABC" for step in steps_of(phase)]:
        if name not in BANKS or (name in ("sum", "var") and n > 0):
            continue
        ring = BANKS[name]
        b = ring[turn.get(ring, 0) % len(ring)]
        turn[ring] = turn.get(ring, 0) + 1
        uses[name, n] = (b, count[b])
        count[b] += 1
    return uses, count


def build_vit_block(nc, ins, out, images):
    with ExitStack() as ctx:
        def sb(name, shape, dt=F32):
            return ctx.enter_context(nc.sbuf_tensor(name, shape, dt))

        signals = {}

        def signal(name, per):
            signals[name] = Signal(ctx.enter_context(nc.semaphore(name)), per)
            return signals[name]

        p1 = sb("p1", [128, H, 2, T])
        p2 = sb("p2", [128, H, 2, T])
        room = [p[0:96].rearrange("p h c t -> p (h c t)") for p in (p1, p2)]
        taken = [0, 0]

        def raw(which, rows, *dims):
            n = int(np.prod(dims))
            ap = room[which][0:rows, taken[which]:taken[which] + n]
            taken[which] += n
            assert taken[which] <= 2 * H * T
            names = "abcd"[:len(dims)]
            return ap.rearrange(f"p ({' '.join(names)}) -> p {' '.join(names)}", **dict(zip(names, dims)))

        basis = raw(1, 72, 2, CH, KC * KR)
        wqk = raw(0, DK, 2, 2 * H, E2)
        wv2_raw = raw(1, DK, 2, H * E2)
        wq1_raw = raw(0, DK, 2, D)
        wk1_raw = raw(0, DK, 2, D)
        wv1_raw = raw(0, DK, 2, D)
        wgate_raw = raw(0, DK, 2, NG)
        proj_tok = sb("proj_tok", [72, 2, CH, D])
        sel_rstd_raw = sb("sel_rstd_raw", [128, H, 128])
        sel_head_raw = sb("sel_head_raw", [128, 6, 128])
        sel_max_raw = sb("sel_max_raw", [128, GROUP, TC])
        ident = sb("ident", [128, 128])
        sel_var = sb("sel_var", [128, H, 32])
        sel_sum = sb("sel_sum", [128, 2, 3, 32])
        sel_rstd = sb("sel_rstd", [128, H, 128], F16)
        sel_head = sb("sel_head", [128, 6, 128], F16)
        sel_max = sb("sel_max", [128, GROUP, TC], BF16)
        mask1 = sb("mask1", [DK, 6])
        iota = sb("iota", [TC, 2, 10])
        center = sb("center", [128, 128])
        freq_h = sb("freq_h", [72, 2])
        freq_w = sb("freq_w", [72, 2])
        weff = sb("weff", [KR, KC, D])
        pos = sb("pos", [TC, 2, D])
        tok_add = sb("tok_add", [TC, 2, D])
        posb = sb("posb", [TC, 2, D])
        wq1 = [sb(f"wq1_{x}", [DK, 2, D], F16) for x in "hl"]
        wk1 = [sb(f"wk1_{x}", [DK, 2, D], F16) for x in "hl"]
        wv1 = [sb(f"wv1_{x}", [DK, 2, D], F16) for x in "hl"]
        wgate = [sb(f"wgate_{x}", [DK, 2, NG], F16) for x in "hl"]
        wqkc = [sb(f"wqkc_{x}", [DK, 2, 2 * H, E2], F16) for x in "hl"]
        wv2 = [sb(f"wv2_{x}", [DK, 2, H * E2], F16) for x in "hl"]
        bq1 = sb("bq1", [DK, 2])
        bk1 = sb("bk1", [DK, 2])
        bv1 = sb("bv1", [TC, D])
        wo1 = sb("wo1", [128, 3, D])
        bo1 = sb("bo1", [TC, D])
        wqk_mean = sb("wqk_mean", [DK, 2, 2 * H])
        bqk = sb("bqk", [128, 2, 6])
        bqkc = sb("bqkc", [128, 2, 6])
        bv2 = sb("bv2", [TC, H * E2])
        ln_w = sb("ln_w", [128, 2])
        ln_b = sb("ln_b", [128, 2])
        wp2 = sb("wp2", [128, 6, D])
        bp2 = sb("bp2", [TC, D])
        mhalf = sb("mhalf", [TC, 2])

        xa = sb("xa", [KR, KC, NPATCH])
        xb = sb("xb", [KR, KC, NPATCH])
        xs = sb("xs", [KR, KC, TP])
        h1 = sb("h1", [TC, 2, D])
        h1b = sb("h1b", [TC, 2, D])
        stats = sb("stats", [TC, 2, 6])
        both = sb("both", [TC, 2, 2])
        apart = sb("apart", [TC, 2])
        mean = sb("mean", [TC, 2])
        vare = sb("vare", [TC, 2])
        rstd = sb("rstd", [TC, 2])
        x1 = sb("x1", [TC, 2, D])
        x1T = [sb(f"x1T_{x}", [DK, 2, TP], F16) for x in "hl"]
        qm1 = sb("qm1", [DK, 2, 6, T])
        kT1 = sb("kT1", [DK, 2, TP])
        v1 = sb("v1", [TC, 2, D])
        nmax1 = sb("nmax1", [TC, 2, H])
        sum1 = sb("sum1", [TC, 2, H])
        rsum1 = sb("rsum1", [TC, 2, H])
        vs1 = sb("vs1", [128, 2, H, 32])
        ctxT = sb("ctxT", [128, 3, TP])
        h2 = sb("h2", [TC, 2, D])
        x2 = x1
        x2T = [sb(f"x2T_{x}", [DK, 2, TP], F16) for x in "hl"]
        h2b = sb("h2b", [TC, 2, D])
        glog = sb("glog", [TC, 2, NG])
        gexp = sb("gexp", [TC, 2, NG])
        gsm = sb("gsm", [TC, 2, NG])
        gtmp = sb("gtmp", [TC, 6, 2, 10])
        gred = sb("gred", [TC, 12, 2, 2])
        mg = sb("mg", [TC, 2, H])
        gates = sb("gates", [TC, 2, 4, 32])
        gT = sb("gT", [128, TP])
        qkc = sb("qkc", [128, 6, 2, TP])
        sq = sb("sq", [128, 6, 2, TP])
        qkn = sq
        var = sb("var", [128, TP])
        rs = sb("rs", [128, TP])
        rs_h = sb("rs_h", [128, TP], F16)
        rs_l = sb("rs_l", [128, TP], F16)
        newton = sb("newton", [128, TP])
        qh = sb("qh", [128, H, TP], F16)
        ql = sb("ql", [128, H, TP], F16)
        kh = sb("kh", [128, 6, TP], F16)
        kl = sb("kl", [128, 6, TP], F16)
        v2 = sb("v2", [128, 2, H * E2])
        max2 = sb("max2", [TC, 2, H])
        maxT = sb("maxT", [128, 3, TP], BF16)
        oT = sb("oT", [128, 6, T])
        rsum2 = sb("rsum2", [128, T])
        gn = sb("gn", [128, T])
        gn_h = sb("gn_h", [128, T], F16)
        gn_l = sb("gn_l", [128, T], F16)
        oS = sb("oS", [128, 6, TP])
        res = sb("res", [TC, 2, D])

        uses, count = bank_uses()
        banks = [Bank(ctx.enter_context(nc.psum_tensor(f"bank{b}", [128, 512], F32)),
                      signal(f"bank{b}_full", count[b]), signal(f"bank{b}_free", count[b])) for b in range(8)]

        def psum(*key):
            return banks[uses[key][0]].tensor

        def room_for(img, *key):
            b, n = uses[key]
            return banks[b].free.at(img, n)

        def made(img, *key):
            b, n = uses[key]
            return banks[b].full.at(img, n + 1)

        def read_out(img, *key):
            b, n = uses[key]
            return banks[b].free.at(img, n + 1)

        def lasts(name, numbers):
            last = {uses[name, n][0]: n for n in numbers}
            return sorted(last.values())

        def full(*key):
            return banks[uses[key][0]].full.up()

        def free(*key):
            return banks[uses[key][0]].free.up()

        s_load = signal("x_loaded", 32)
        s_fold = signal("xs_folded", 1)
        s_mv = signal("mean_var_ready", 2)
        s_rstd = signal("rstd_ready", 2)
        s_x1 = signal("x1_ready", 1)
        s_h1b = signal("h1_bias_ready", 1)
        s_x1h = signal("x1T_high_ready", 1)
        s_nm = signal("max1_ready", H)
        s_vs = signal("v1_scaled", 3)
        s_x2 = signal("x2_ready", 1)
        s_x2h = signal("x2T_high_ready", 1)
        s_h2b = signal("h2_bias_ready", 1)
        s_gmax = signal("gate_logits_shifted", 1)
        s_gexp = signal("gate_exp_ready", 1)
        s_gate = signal("gates_ready", 1)
        s_sq = signal("qk_squared", 6)
        s_rs = signal("head_rstd_ready", 1)
        s_hi = signal("qk_high_parts", 6)
        s_lo = signal("qk_low_parts", 6)
        s_gn = signal("gate_over_sum_ready", 1)
        s_out = signal("stored", 32)
        s_step_a = signal("vector_step_a", 9)
        s_step_b = signal("vector_step_b", 35)
        s_step_c = signal("vector_step_c", 2)
        s_w = ctx.enter_context(nc.semaphore("weights_loaded"))
        s_const = ctx.enter_context(nc.semaphore("weights_prepared"))
        s_pool = ctx.enter_context(nc.semaphore("padding_zeroed"))
        s_prep = ctx.enter_context(nc.semaphore("prep_vector_step"))
        s_pw = ctx.enter_context(nc.semaphore("token_weights_scaled"))
        s_weff = ctx.enter_context(nc.semaphore("token_weights_in_psum"))

        block = ctx.enter_context(nc.Block())

        loads = [(basis, "basis"), (proj_tok[:], "proj_tok"), (freq_h[:], "freq_h"), (freq_w[:], "freq_w"),
                 (center[:], "center"), (bqk[:], "bqk"), (wqk, "wqk"), (wq1_raw, "wq1"), (wk1_raw, "wk1"),
                 (wv1_raw, "wv1"), (wgate_raw, "wgate"), (wv2_raw, "wv2"), (sel_rstd_raw[:], "sel_rstd"),
                 (sel_head_raw[:], "sel_head"), (sel_max_raw[:], "sel_max"), (ident[:], "ident"),
                 (sel_var[:], "sel_var"), (sel_sum[:], "sel_sum"), (mask1[:], "mask1"), (iota[:], "iota"),
                 (pos[:], "pos"), (tok_add[:], "tok_add"), (bq1[:], "bq1"), (bk1[:], "bk1"), (bv1[:], "bv1"),
                 (wo1[:], "wo1"), (bo1[:], "bo1"), (bv2[:], "bv2"), (ln_w[:], "ln_w"), (ln_b[:], "ln_b"),
                 (wp2[:], "wp2"), (bp2[:], "bp2")]

        def run_phases(eng, steps):
            def go(phases, image):
                for phase, name, n in steps_of(phases):
                    if name in steps:
                        steps[name](image[phase], n)

            go("A", {"A": 0})
            go("AB", {"A": 1, "B": 0})
            go("ABC", {"A": 2, "B": 1, "C": 0})
            with eng.Fori(1, images - 2) as i:
                go("ABC", {"A": i + 2, "B": i + 1, "C": i})
            go("BC", {"B": images - 1, "C": images - 2})
            go("C", {"C": images - 1})

        @block.sync
        def _(sp):
            for dst, name in loads:
                sp.dma_start(dst, ins[name]).then_inc(s_w, 16)

            def load(img):
                sp.wait_ge(*s_fold.at(img, 0))
                sp.dma_start(xa[:], ins["xa"][bass.ds(img, 1)].rearrange("b p k n -> (b p) k n")).then_inc(s_load.up(16), 16)
                sp.dma_start(xb[:], ins["xb"][bass.ds(img, 1)].rearrange("b p k n -> (b p) k n")).then_inc(s_load.up(16), 16)

            def store(img):
                sp.wait_ge(*read_out(img, "proj", 0))
                dst = out[bass.ds(img, 1)].rearrange("b t d -> (b t) d")
                sp.dma_start(dst[0:TC, :], res[:, 0, :]).then_inc(s_out.up(16), 16)
                sp.dma_start(dst[TC:T, :], res[0:T - TC, 1, :]).then_inc(s_out.up(16), 16)

            load(0)
            load(1)
            load(2)
            store(0)
            with sp.Fori(1, images - 2) as i:
                load(i + 2)
                store(i)
            store(images - 2)
            store(images - 1)
            sp.wait_ge(s_out.sem, s_out.per * images)

        @block.gpsimd
        def _(pool):
            nc.gpsimd.memset(p1[96:128], 0.0).then_inc(s_pool, 1)
            nc.gpsimd.memset(p2[96:128], 0.0).then_inc(s_pool, 1)
            pool.wait_ge(s_const, PREPARED)

            def inverse_root(img, layer):
                pool.wait_ge(*s_mv.at(img, layer + 1))
                nc.gpsimd.tensor_tensor(rstd[:], vare[:], mhalf[:], op=ALU.pow).then_inc(s_rstd.up(), 1)

            def tok(img, _):
                inverse_root(img, 0)
                pool.wait_ge(*read_out(img, "tok", 0))
                for c in range(2):
                    last = nc.gpsimd.tensor_tensor(h1b[:, c, :], h1[:, c, :], bo1[:], op=ALU.add)
                last.then_inc(s_h1b.up(), 1)

            def wo(img, _):
                inverse_root(img, 1)

            def h2b_(img, _):
                pool.wait_ge(*read_out(img, "wo", 0))
                pool.wait_ge(*banks[uses["proj", 0][0]].free.at(img, 0))
                for c in range(2):
                    last = nc.gpsimd.tensor_tensor(h2b[:, c, :], h2[:, c, :], bp2[:], op=ALU.add)
                last.then_inc(s_h2b.up(), 1)

            run_phases(pool, {"tok": tok, "wo": wo, "h2b": h2b_})

        @block.tensor
        def _(pe):
            def mm(o, l, r, first=True, last=True):
                return nc.tensor.matmul(o, l, r, start=first, stop=last)

            def mm3(o, l, r, first=True, last=True):
                mm(o, l[0], r[0], first, False)
                mm(o, l[1], r[0], False, False)
                return mm(o, l[0], r[1], False, last)

            pe.wait_ge(s_w, 16 * len(loads))
            pe.wait_ge(s_pw, 1)
            for k in range(KC):
                for n in range(6):
                    c, a = divmod(n, 2)
                    mm(banks[k].tensor[0:KR, 0:D], basis[:, a, c, KR * k:KR * k + KR], proj_tok[:, a, c, :], n == 0, n == 5)
            mm(banks[4].tensor[:, 0:12], center[:], bqk[:].rearrange("p s t -> p (s t)")).then_inc(s_weff, 1)
            pe.wait_ge(s_const, PREPARED)
            pe.wait_ge(s_pool, 2)

            def tok(img, _):
                o = psum("tok", 0)
                pe.wait_ge(*room_for(img, "tok", 0))
                pe.wait_ge(*s_fold.at(img, 1))
                for c in range(2):
                    for k in range(KC):
                        last = mm(o[0:TC, c * D:c * D + D], xs[:, k, c * TC:c * TC + TC], weff[:, k, :], k == 0, k == KC - 1)
                last.then_inc(full("tok", 0), 1)

            def transposes(o, src):
                for kc in range(2):
                    for c in range(2):
                        last = nc.tensor.transpose(o[0:DK, kc * TP + c * TC:kc * TP + c * TC + TC],
                                                   src[:, c, kc * DK:kc * DK + DK], ident[0:TC, 0:TC])
                return last

            def x1T_(img, _):
                pe.wait_ge(*room_for(img, "x1T", 0))
                pe.wait_ge(*s_x1.at(img, 1))
                transposes(psum("x1T", 0), x1).then_inc(full("x1T", 0), 1)

            def x2T_(img, _):
                pe.wait_ge(*room_for(img, "x2T", 0))
                pe.wait_ge(*s_x2.at(img, 1))
                transposes(psum("x2T", 0), x2).then_inc(full("x2T", 0), 1)

            def project1(img, key, w):
                o = psum(key, 0)
                pe.wait_ge(*room_for(img, key, 0))
                pe.wait_ge(*read_out(img, "x1T", 0))
                for t in range(2):
                    for kc in range(2):
                        last = mm3(o[0:DK, t * TP:t * TP + TP], [x[:, kc, t * DK:t * DK + DK] for x in w],
                                   [x[:, kc, :] for x in x1T], kc == 0, kc == 1)
                last.then_inc(full(key, 0), 1)

            def q1(img, _):
                project1(img, "q1", wq1)

            def k1(img, _):
                project1(img, "k1", wk1)

            def v1_(img, _):
                o = psum("v1", 0)
                pe.wait_ge(*room_for(img, "v1", 0))
                pe.wait_ge(*read_out(img, "x1T", 0))
                for c in range(2):
                    for kc in range(2):
                        last = mm3(o[0:TC, c * D:c * D + D], [x[:, kc, c * TC:c * TC + TC] for x in x1T],
                                   [x[:, kc, :] for x in wv1], kc == 0, kc == 1)
                last.then_inc(full("v1", 0), 1)

            def s1(img, h):
                t, j = divmod(h, 6)
                o = psum("s1", h)
                pe.wait_ge(*room_for(img, "s1", h))
                if h == 0:
                    pe.wait_ge(*read_out(img, "k1", 0))
                    pe.wait_ge(*read_out(img, "q1", 0))
                for c in range(2):
                    last = mm(o[0:TC, c * T:c * T + T], kT1[:, t, c * TC:c * TC + TC], qm1[:, t, j, :])
                last.then_inc(full("s1", h), 1)

            def ctx_(img, g):
                o = psum("ctx", g)
                pe.wait_ge(*room_for(img, "ctx", g))
                pe.wait_ge(*s_vs.at(img, g + 1))
                for h in lasts("s1", range(GROUP * g, GROUP * g + GROUP)):
                    pe.wait_ge(*read_out(img, "s1", h))
                for c in range(2):
                    for j in range(GROUP):
                        h = GROUP * g + j
                        last = mm(o[32 * j:32 * j + 32, 0:T], vs1[:, c, h, :], p1[:, h, c, :], c == 0, c == 1)
                last.then_inc(full("ctx", g), 1)

            def wo(img, _):
                o = psum("wo", 0)
                pe.wait_ge(*room_for(img, "wo", 0))
                pe.wait_ge(*read_out(img, "ctx", 2))
                for c in range(2):
                    for g in range(3):
                        last = mm(o[0:TC, c * D:c * D + D], ctxT[:, g, c * TC:c * TC + TC], wo1[:, g, :], g == 0, g == 2)
                last.then_inc(full("wo", 0), 1)

            def gl(img, _):
                o = psum("gl", 0)
                pe.wait_ge(*room_for(img, "gl", 0))
                pe.wait_ge(*read_out(img, "x2T", 0))
                for c in range(2):
                    for kc in range(2):
                        last = mm3(o[0:TC, c * NG:c * NG + NG], [x[:, kc, c * TC:c * TC + TC] for x in x2T],
                                   [x[:, kc, :] for x in wgate], kc == 0, kc == 1)
                last.then_inc(full("gl", 0), 1)

            def mean_square(img, t):
                if t == 0:
                    pe.wait_ge(*room_for(img, "var", 0))
                pe.wait_ge(*s_sq.at(img, t + 1))
                for s in range(2):
                    u = 2 * t + s
                    q = 32 * (u % 4)
                    last = mm(psum("var", 0)[q:q + 32, 0:TP], sel_var[:, u, :], sq[:, t, s, :], u < 4, u >= 8)
                if t == 5:
                    last.then_inc(full("var", 0), 1)

            def qk(img, t):
                o = psum("qk", t)
                pe.wait_ge(*room_for(img, "qk", t))
                pe.wait_ge(*read_out(img, "x2T", 0))
                for s in range(2):
                    for kc in range(2):
                        w = [x[:, kc, H * s + 2 * t:H * s + 2 * t + 2, :].rearrange("p a b -> p (a b)") for x in wqkc]
                        last = mm3(o[:, s * TP:s * TP + TP], w, [x[:, kc, :] for x in x2T], kc == 0, kc == 1)
                last.then_inc(full("qk", t), 1)

            def v2_(img, n):
                c, a = divmod(n, 2)
                o = psum("v2", n)
                pe.wait_ge(*room_for(img, "v2", n))
                for kc in range(2):
                    last = mm3(o[0:TC, 0:384], [x[:, kc, c * TC:c * TC + TC] for x in x2T],
                               [x[:, kc, 384 * a:384 * a + 384] for x in wv2], kc == 0, kc == 1)
                last.then_inc(full("v2", n), 1)

            def rstd_(img, t):
                o = psum("rstd", t)
                pe.wait_ge(*room_for(img, "rstd", t))
                pe.wait_ge(*s_rs.at(img, 1))
                for s in range(2):
                    mm(o[:, s * TP:s * TP + TP], sel_rstd[:, 2 * t + s, :], rs_h[:], True, False)
                    last = mm(o[:, s * TP:s * TP + TP], sel_rstd[:, 2 * t + s, :], rs_l[:], False, True)
                last.then_inc(full("rstd", t), 1)

            def gT_(img, _):
                pe.wait_ge(*room_for(img, "gT", 0))
                pe.wait_ge(*s_gate.at(img, 1))
                for c in range(2):
                    last = nc.tensor.transpose(psum("gT", 0)[:, c * TC:c * TC + TC], gates[:, c].rearrange("p a b -> p (a b)"),
                                               ident[0:TC, 0:TC])
                last.then_inc(full("gT", 0), 1)

            def smax(img, h):
                o = psum("smax", h)
                pe.wait_ge(*room_for(img, "smax", h))
                pe.wait_ge(*s_hi.at(img, h // 2 + 1))
                for c in range(2):
                    last = mm(o[0:TC, c * T:c * T + T], qh[:, h, c * TC:c * TC + TC], kh[:, h // 2, 0:T])
                last.then_inc(full("smax", h), 1)

            def maxT_(img, g):
                pe.wait_ge(*room_for(img, "maxT", g))
                for h in lasts("smax", range(GROUP * g, GROUP * g + GROUP)):
                    pe.wait_ge(*read_out(img, "smax", h))
                for c in range(2):
                    last = nc.tensor.transpose(psum("maxT", g)[0:GROUP, c * TC:c * TC + TC],
                                               max2[:, c, GROUP * g:GROUP * g + GROUP], ident[0:TC, 0:TC])
                last.then_inc(full("maxT", g), 1)

            def s2(img, h):
                g, j, t = h // GROUP, h % GROUP, h // 2
                o = psum("s2", h)
                pe.wait_ge(*room_for(img, "s2", h))
                pe.wait_ge(*read_out(img, "maxT", g))
                pe.wait_ge(*s_lo.at(img, t + 1))
                for c in range(2):
                    cols = slice(c * TC, c * TC + TC)
                    oc = o[0:TC, c * T:c * T + T]
                    mm3(oc, (kh[:, t, cols], kl[:, t, cols]), (qh[:, h, 0:T], ql[:, h, 0:T]), True, False)
                    last = mm(oc, sel_max[:, j, :], maxT[:, g, 0:T], False, True)
                last.then_inc(full("s2", h), 1)

            def o2(img, t):
                o = psum("o2", t)
                pe.wait_ge(*room_for(img, "o2", t))
                if t == 0:
                    for n in lasts("v2", range(4)):
                        if uses["v2", n][0] != uses["o2", 0][0]:
                            pe.wait_ge(*read_out(img, "v2", n))
                for h in lasts("s2", (2 * t, 2 * t + 1)):
                    pe.wait_ge(*read_out(img, "s2", h))
                for c in range(2):
                    for j in range(2):
                        h = 2 * t + j
                        last = mm(o[64 * j:64 * j + 64, 0:T], v2[:, c, E2 * h:E2 * h + E2], p2[:, h, c, :], c == 0, c == 1)
                last.then_inc(full("o2", t), 1)

            def sum_(img, g):
                if g == 0:
                    pe.wait_ge(*room_for(img, "sum", 0))
                for h in lasts("s2", range(GROUP * g, GROUP * g + GROUP)):
                    pe.wait_ge(*read_out(img, "s2", h))
                for c in range(2):
                    for j in range(GROUP):
                        last = mm(psum("sum", 0)[32 * j:32 * j + 32, 0:T], sel_sum[:, c, g, :], p2[:, GROUP * g + j, c, :],
                                  g == 0 and c == 0, g == 2 and c == 1)
                if g == 2:
                    last.then_inc(full("sum", 0), 1)

            def gh(img, t):
                o = psum("gh", t)
                pe.wait_ge(*room_for(img, "gh", t))
                pe.wait_ge(*s_gn.at(img, 1))
                mm(o[:, 0:T], sel_head[:, t, :], gn_h[:], True, False)
                mm(o[:, 0:T], sel_head[:, t, :], gn_l[:], False, True).then_inc(full("gh", t), 1)

            def proj(img, _):
                o = psum("proj", 0)
                pe.wait_ge(*room_for(img, "proj", 0))
                for t in lasts("gh", range(6)):
                    pe.wait_ge(*read_out(img, "gh", t))
                for c in range(2):
                    for t in range(6):
                        last = mm(o[0:TC, c * D:c * D + D], oS[:, t, c * TC:c * TC + TC], wp2[:, t, :], t == 0, t == 5)
                last.then_inc(full("proj", 0), 1)

            run_phases(pe, {"tok": tok, "x1T": x1T_, "q1": q1, "k1": k1, "v1": v1_, "s1": s1, "ctx": ctx_, "wo": wo, "x2T": x2T_, "gl": gl,
                            "qk": qk, "ms": mean_square, "v2": v2_, "rstd": rstd_, "gT": gT_, "smax": smax, "maxT": maxT_, "s2": s2,
                            "o2": o2, "sum": sum_, "gh": gh, "proj": proj})

        @block.scalar
        def _(act):
            act.wait_ge(s_const, PREPARED)
            act.wait_ge(s_pool, 2)

            def x1T_(img, _):
                act.wait_ge(*made(img, "x1T", 0))
                nc.scalar.activation(x1T[0][:].rearrange("p a b -> p (a b)"), psum("x1T", 0)[0:DK, 0:2 * TP],
                                     ACT.Copy).then_inc(s_x1h.up(), 1)

            def x2T_(img, _):
                act.wait_ge(*made(img, "x2T", 0))
                nc.scalar.activation(x2T[0][:].rearrange("p a b -> p (a b)"), psum("x2T", 0)[0:DK, 0:2 * TP],
                                     ACT.Copy).then_inc(s_x2h.up(), 1)

            def k1(img, _):
                act.wait_ge(*made(img, "k1", 0))
                for t in range(2):
                    last = nc.scalar.activation(kT1[:, t, :], psum("k1", 0)[0:DK, t * TP:t * TP + TP], ACT.Identity,
                                                bias=bk1[:, t:t + 1], scale=1.0 / W_SCALE)
                last.then_inc(free("k1", 0), 1)

            def s1(img, h):
                act.wait_ge(*made(img, "s1", h))
                act.wait_ge(*s_nm.at(img, h + 1))
                for c in range(2):
                    last = nc.scalar.activation(p1[0:TC, h, c, :], psum("s1", h)[0:TC, c * T:c * T + T], ACT.Exp,
                                                bias=nmax1[:, c, h:h + 1], accum_out=sum1[:, c, h:h + 1])
                last.then_inc(free("s1", h), 1)

            def ctx_(img, g):
                act.wait_ge(*made(img, "ctx", g))
                nc.scalar.activation(ctxT[:, g, 0:T], psum("ctx", g)[:, 0:T], ACT.Copy).then_inc(free("ctx", g), 1)

            def qk(img, t):
                act.wait_ge(*made(img, "qk", t))
                for s in range(2):
                    last = nc.scalar.activation(qkc[:, t, s, :], psum("qk", t)[:, s * TP:s * TP + TP], ACT.Identity,
                                                bias=bqkc[:, s, t:t + 1], scale=1.0 / W_SCALE)
                last.then_inc(free("qk", t), 1)
                act.wait_ge(*read_out(img, "qk", t))
                nc.scalar.activation(sq[:, t], qkc[:, t], ACT.Square).then_inc(s_sq.up(), 1)

            def gate(img, n):
                if n != 1:
                    return
                act.wait_ge(*s_gmax.at(img, 1))
                nc.scalar.activation(gexp[:], glog[:], ACT.Exp).then_inc(s_gexp.up(), 1)

            def rstd_(img, t):
                act.wait_ge(*read_out(img, "rstd", t))
                for j in range(2):
                    r = slice(64 * j, 64 * j + 64)
                    nc.scalar.activation(qh[r, 2 * t + j, :], qkn[r, t, 0, :], ACT.Identity, bias=ln_b[r, 0:1])
                nc.scalar.activation(kh[:, t, :], qkn[:, t, 1, :], ACT.Identity, bias=ln_b[:, 1:2]).then_inc(s_hi.up(), 1)

            def maxT_(img, g):
                act.wait_ge(*made(img, "maxT", g))
                nc.scalar.activation(maxT[0:GROUP, g, :], psum("maxT", g)[0:GROUP, 0:TP], ACT.Copy).then_inc(free("maxT", g), 1)

            def s2(img, h):
                act.wait_ge(*made(img, "s2", h))
                nc.scalar.activation(p2[0:TC, h].rearrange("p a b -> p (a b)"), psum("s2", h)[0:TC, 0:2 * T], ACT.Exp,
                                     scale=E2 ** -0.5).then_inc(free("s2", h), 1)

            def o2(img, t):
                act.wait_ge(*made(img, "o2", t))
                nc.scalar.activation(oT[:, t, :], psum("o2", t)[:, 0:T], ACT.Copy).then_inc(free("o2", t), 1)

            run_phases(act, {"x1T": x1T_, "k1": k1, "s1": s1, "ctx": ctx_, "x2T": x2T_, "gate": gate, "qk": qk,
                             "rstd": rstd_, "maxT": maxT_, "s2": s2, "o2": o2})

        @block.vector
        def _(dve):
            V = nc.vector
            dve.wait_ge(s_w, 16 * len(loads))
            prep = [0]

            def link(ins_):
                prep[0] += 1
                ins_.then_inc(s_prep, 1)
                dve.wait_ge(s_prep, prep[0])

            for a in range(2):
                v = proj_tok[:, a].rearrange("p c d -> p (c d)")
                link(V.tensor_scalar(v, v, freq_h[:, a:a + 1], freq_w[:, a:a + 1], ALU.mult, ALU.mult))
            V.memset(xs[:], 0.0).then_inc(s_pw, 1)
            link(V.tensor_reduce(wqk_mean[:], wqk, op=ALU.add, axis=AX.X))
            link(V.tensor_scalar(wqk_mean[:], wqk_mean[:], 1.0 / E2, None, ALU.mult))
            for kc in range(2):
                link(V.tensor_tensor(wqk[:, kc], wqk[:, kc], wqk_mean[:, kc].unsqueeze(2).to_broadcast([DK, 2 * H, E2]),
                                     op=ALU.subtract))
            for source, parts in ((wqk, wqkc), (wv2_raw, wv2), (wq1_raw, wq1), (wk1_raw, wk1), (wv1_raw, wv1), (wgate_raw, wgate)):
                whole = "p a b c -> p (a b c)" if len(source.shape) == 4 else "p a b -> p (a b)"
                high, low = (x[:].rearrange(whole) for x in parts)
                source = source.rearrange(whole)
                link(V.tensor_scalar(high, source, W_SCALE, None, ALU.mult))
                link(V.scalar_tensor_tensor(low, source, W_SCALE, high, ALU.mult, ALU.subtract))
            for x in (bq1,):
                link(V.tensor_scalar(x[:], x[:], W_SCALE, None, ALU.mult))
            link(V.tensor_tensor(posb[:], pos[:], tok_add[:], op=ALU.add))
            link(V.tensor_copy(sel_max[:], sel_max_raw[:]))
            link(V.tensor_copy(sel_rstd[:], sel_rstd_raw[:]))
            link(V.tensor_copy(sel_head[:], sel_head_raw[:]))
            for x in (mhalf,):
                link(V.memset(x[:], -0.5))
            for x in (vs1, ctxT, gates, qh, ql, maxT, oS, v2):
                link(V.memset(x[:], 0.0))
            dve.wait_ge(s_weff, 1)
            link(V.tensor_copy(bqkc[:].rearrange("p s t -> p (s t)"), banks[4].tensor[:, 0:12]))
            for k in range(KC):
                link(V.tensor_copy(weff[:, k, :], banks[k].tensor[0:KR, 0:D]))
            V.memset(gtmp[:], 0.0).then_inc(s_const, PREPARED)
            dve.wait_ge(s_const, PREPARED)

            def step_a(ins_, img):
                ins_.then_inc(s_step_a.up(), 1)
                dve.wait_ge(*s_step_a.at(img, (s_step_a.made - 1) % s_step_a.per + 1))

            def step_b(ins_, img):
                ins_.then_inc(s_step_b.up(), 1)
                dve.wait_ge(*s_step_b.at(img, (s_step_b.made - 1) % s_step_b.per + 1))

            def step_c(ins_, img):
                ins_.then_inc(s_step_c.up(), 1)
                dve.wait_ge(*s_step_c.at(img, (s_step_c.made - 1) % s_step_c.per + 1))

            def moments(img, src):
                for c in range(2):
                    last = V.bn_stats(stats[:, c, :], src[:, c, :])
                step_a(last, img)
                halves = stats[:].rearrange("p c (o s) -> p c o s", o=2)
                V.tensor_tensor(both[:], halves[:, :, 0, 1:3], halves[:, :, 1, 1:3], op=ALU.add)
                step_a(V.tensor_tensor(apart[:], halves[:, :, 0, 1], halves[:, :, 1, 1], op=ALU.subtract), img)
                V.tensor_scalar(mean[:], both[:, :, 0], 0.5, None, ALU.mult)
                V.tensor_scalar(vare[:], both[:, :, 1], 1.0 / D, LN_EPS, ALU.mult, ALU.add)
                step_a(V.tensor_tensor(apart[:], apart[:], apart[:], op=ALU.mult), img)
                V.scalar_tensor_tensor(vare[:], apart[:], 0.25, vare[:], ALU.mult, ALU.add).then_inc(s_mv.up(), 1)

            def normalise(img, src, dst, sig, n):
                dve.wait_ge(*s_rstd.at(img, n))
                for c in range(2):
                    last = V.tensor_scalar(dst[:, c, :], src[:, c, :], mean[:, c:c + 1], rstd[:, c:c + 1], ALU.subtract, ALU.mult)
                last.then_inc(sig.up(), 1)

            def fold(img, _):
                dve.wait_ge(*s_load.at(img, 32))
                V.tensor_tensor(xs[:, :, 1:T], xa[:], xb[:], op=ALU.add).then_inc(s_fold.up(), 1)

            def tok(img, _):
                dve.wait_ge(*made(img, "tok", 0))
                dve.wait_ge(*s_h1b.at(img, 0))
                V.tensor_tensor(h1[:].rearrange("p a b -> p (a b)"), psum("tok", 0)[0:TC, 0:2 * D],
                                posb[:].rearrange("p a b -> p (a b)"), op=ALU.add).then_inc(free("tok", 0), 1)
                dve.wait_ge(*read_out(img, "tok", 0))
                moments(img, h1)

            def nx1(img, _):
                normalise(img, h1, x1, s_x1, 1)

            def x1T_(img, _):
                dve.wait_ge(*s_x1h.at(img, 1))
                V.tensor_tensor(x1T[1][:].rearrange("p a b -> p (a b)"), psum("x1T", 0)[0:DK, 0:2 * TP],
                                x1T[0][:].rearrange("p a b -> p (a b)"), op=ALU.subtract).then_inc(free("x1T", 0), 1)

            def q1(img, _):
                dve.wait_ge(*made(img, "q1", 0))
                for t in range(2):
                    last = V.scalar_tensor_tensor(qm1[:, t], psum("q1", 0)[0:DK, t * TP:t * TP + T].unsqueeze(1).to_broadcast([DK, 6, T]),
                                                  bq1[:, t:t + 1], mask1[:].unsqueeze(2).to_broadcast([DK, 6, T]), ALU.add, ALU.mult)
                last.then_inc(free("q1", 0), 1)

            def v1_(img, _):
                dve.wait_ge(*made(img, "v1", 0))
                V.scalar_tensor_tensor(v1[:], psum("v1", 0)[0:TC, 0:2 * D].rearrange("p (a b) -> p a b", a=2), 1.0 / W_SCALE,
                                       bv1[:].unsqueeze(1).to_broadcast([TC, 2, D]), ALU.mult, ALU.add).then_inc(free("v1", 0), 1)

            def s1(img, h):
                dve.wait_ge(*made(img, "s1", h))
                V.tensor_reduce(nmax1[:, :, h], psum("s1", h)[0:TC, 0:2 * T].rearrange("p (a b) -> p a b", a=2),
                                op=ALU.max, axis=AX.X, negate=True).then_inc(s_nm.up(), 1)

            def ctx_(img, g):
                hs = slice(GROUP * g, GROUP * g + GROUP)
                for h in lasts("s1", range(GROUP * g, GROUP * g + GROUP)):
                    dve.wait_ge(*read_out(img, "s1", h))
                step_a(V.reciprocal(rsum1[:, :, hs], sum1[:, :, hs]), img)
                dve.wait_ge(*read_out(img, "v1", 0))
                for c in range(2):
                    n = TC - c
                    last = V.tensor_tensor(vs1[0:n, c, hs, 0:E1],
                                           v1[0:n, c, E1 * GROUP * g:E1 * GROUP * (g + 1)].rearrange("p (h e) -> p h e", h=GROUP),
                                           rsum1[0:n, c, hs].unsqueeze(2).to_broadcast([n, GROUP, E1]), op=ALU.mult)
                last.then_inc(s_vs.up(), 1)

            def wo(img, _):
                dve.wait_ge(*made(img, "wo", 0))
                dve.wait_ge(*s_h1b.at(img, 1))
                dve.wait_ge(*s_h2b.at(img, 0))
                V.tensor_tensor(h2[:].rearrange("p a b -> p (a b)"), psum("wo", 0)[0:TC, 0:2 * D],
                                h1b[:].rearrange("p a b -> p (a b)"), op=ALU.add).then_inc(free("wo", 0), 1)
                dve.wait_ge(*read_out(img, "wo", 0))
                moments(img, h2)

            def nx2(img, _):
                normalise(img, h2, x2, s_x2, 2)

            def x2T_(img, _):
                dve.wait_ge(*s_x2h.at(img, 1))
                V.tensor_tensor(x2T[1][:].rearrange("p a b -> p (a b)"), psum("x2T", 0)[0:DK, 0:2 * TP],
                                x2T[0][:].rearrange("p a b -> p (a b)"), op=ALU.subtract).then_inc(free("x2T", 0), 1)

            def pairs(x):
                return x[:, :, 10:14].rearrange("p c (a b) -> p c a b", b=2)

            routed = gsm[:, :, 0:10]

            def gl(img, _):
                dve.wait_ge(*made(img, "gl", 0))
                V.tensor_scalar(gsm[:].rearrange("p a b -> p (a b)"), psum("gl", 0)[0:TC, 0:2 * NG], 1.0 / W_SCALE, None,
                                ALU.mult).then_inc(free("gl", 0), 1)

            def first_best(img, src, n):
                step_b(V.tensor_reduce(gred[:, 6 + 2 * n, :, 0], src, op=ALU.max, axis=AX.X), img)
                step_b(V.tensor_tensor(gtmp[:, 2 + n], src, gred[:, 6 + 2 * n, :, 0:1].to_broadcast([TC, 2, 10]), op=ALU.is_equal), img)
                step_b(V.scalar_tensor_tensor(gtmp[:, 2 + n], gtmp[:, 2 + n], -100.0, iota[:], ALU.mult, ALU.add), img)
                step_b(V.tensor_reduce(gred[:, 7 + 2 * n, :, 0], gtmp[:, 2 + n], op=ALU.min, axis=AX.X), img)
                step_b(V.tensor_tensor(gtmp[:, n], gtmp[:, 2 + n], gred[:, 7 + 2 * n, :, 0:1].to_broadcast([TC, 2, 10]), op=ALU.is_equal), img)

            def gate(img, n):
                if n == 0:
                    dve.wait_ge(*read_out(img, "gl", 0))
                    V.tensor_reduce(gred[:, 0, :, 0], routed, op=ALU.max, axis=AX.X)
                    step_b(V.tensor_reduce(gred[:, 1], pairs(gsm), op=ALU.max, axis=AX.X), img)
                    V.tensor_tensor(glog[:, :, 0:10], routed, gred[:, 0, :, 0:1].to_broadcast([TC, 2, 10]), op=ALU.subtract)
                    V.tensor_tensor(pairs(glog), pairs(gsm), gred[:, 1].unsqueeze(3).to_broadcast([TC, 2, 2, 2]),
                                    op=ALU.subtract).then_inc(s_gmax.up(), 1)
                if n == 1:
                    dve.wait_ge(*s_gexp.at(img, 1))
                    V.tensor_reduce(gred[:, 2, :, 0], gexp[:, :, 0:10], op=ALU.add, axis=AX.X)
                    step_b(V.tensor_reduce(gred[:, 3], pairs(gexp), op=ALU.add, axis=AX.X), img)
                    V.reciprocal(gred[:, 4, :, 0], gred[:, 2, :, 0])
                    step_b(V.reciprocal(gred[:, 5], gred[:, 3]), img)
                    V.tensor_tensor(routed, gexp[:, :, 0:10], gred[:, 4, :, 0:1].to_broadcast([TC, 2, 10]), op=ALU.mult)
                    step_b(V.tensor_tensor(pairs(gsm), pairs(gexp), gred[:, 5].unsqueeze(3).to_broadcast([TC, 2, 2, 2]), op=ALU.mult), img)
                if n == 2:
                    first_best(img, routed, 0)
                    step_b(V.scalar_tensor_tensor(gtmp[:, 4], gtmp[:, 0], -4.0, routed, ALU.mult, ALU.add), img)
                    first_best(img, gtmp[:, 4], 1)
                if n == 3:
                    step_b(V.tensor_tensor(gtmp[:, 5], gtmp[:, 0], gtmp[:, 1], op=ALU.add), img)
                    step_b(V.tensor_tensor(gtmp[:, 4], gtmp[:, 5], routed, op=ALU.mult), img)
                    step_b(V.tensor_reduce(gred[:, 10, :, 0], gtmp[:, 4], op=ALU.add, axis=AX.X), img)
                    step_b(V.tensor_scalar(gred[:, 10, :, 0], gred[:, 10, :, 0], GATE_EPS, None, ALU.max), img)
                    step_b(V.reciprocal(gred[:, 10, :, 1], gred[:, 10, :, 0]), img)
                    step_b(V.tensor_scalar(gred[:, 11], gsm[:, :, 12:14], 4.0, None, ALU.mult), img)
                    step_b(V.tensor_tensor(gred[:, 10, :, 0], gred[:, 10, :, 1], gred[:, 11, :, 1], op=ALU.mult), img)
                    V.tensor_tensor(mg[:, :, 2:H], gtmp[:, 4], gred[:, 10, :, 0:1].to_broadcast([TC, 2, 10]), op=ALU.mult)
                    step_b(V.tensor_tensor(mg[:, :, 0:2], gsm[:, :, 10:12], gred[:, 11, :, 0:1].to_broadcast([TC, 2, 2]), op=ALU.mult), img)
                    V.tensor_copy(gates[:, :, :, 0:3].rearrange("p c j a -> p c a j"),
                                  mg[:].rearrange("p c (a j) -> p c a j", j=GROUP)).then_inc(s_gate.up(), 1)

            def v2_(img, n):
                c, a = divmod(n, 2)
                dve.wait_ge(*made(img, "v2", n))
                V.scalar_tensor_tensor(v2[0:TC - c, c, 384 * a:384 * a + 384], psum("v2", n)[0:TC - c, 0:384], 1.0 / W_SCALE,
                                       bv2[0:TC - c, 384 * a:384 * a + 384], ALU.mult, ALU.add).then_inc(free("v2", n), 1)

            def var_(img, n):
                if n == 0:
                    dve.wait_ge(*made(img, "var", 0))
                    V.tensor_scalar(var[:], psum("var", 0)[:, 0:TP], LN_EPS, None, ALU.add).then_inc(free("var", 0), 1)
                    dve.wait_ge(*read_out(img, "var", 0))
                    step_b(V.tensor_scalar(rs[:].bitcast(I32), var[:].bitcast(I32), 1, None, ALU.logical_shift_right), img)
                    step_b(V.tensor_scalar(rs[:].bitcast(I32), rs[:].bitcast(I32), -1.0, RSQRT_GUESS, ALU.mult, ALU.add), img)
                elif n < 4:
                    step_b(V.tensor_tensor(newton[:], rs[:], rs[:], op=ALU.mult), img)
                    step_b(V.scalar_tensor_tensor(newton[:], newton[:], -0.5, var[:], ALU.mult, ALU.mult), img)
                    step_b(V.scalar_tensor_tensor(rs[:], newton[:], 1.5, rs[:], ALU.add, ALU.mult), img)
                else:
                    step_b(V.tensor_copy(rs_h[:], rs[:]), img)
                    V.tensor_tensor(rs_l[:], rs[:], rs_h[:], op=ALU.subtract).then_inc(s_rs.up(), 1)

            def low_parts(img, t):
                dve.wait_ge(*s_hi.at(img, t + 1))
                for j in range(2):
                    r = slice(64 * j, 64 * j + 64)
                    V.scalar_tensor_tensor(ql[r, 2 * t + j, :], qkn[r, t, 0, :], ln_b[r, 0:1], qh[r, 2 * t + j, :],
                                           ALU.add, ALU.subtract)
                V.scalar_tensor_tensor(kl[:, t, :], qkn[:, t, 1, :], ln_b[:, 1:2], kh[:, t, :],
                                       ALU.add, ALU.subtract).then_inc(s_lo.up(), 1)

            def rstd_(img, t):
                dve.wait_ge(*made(img, "rstd", t))
                dve.wait_ge(*read_out(img, "qk", t))
                for s in range(2):
                    last = V.scalar_tensor_tensor(qkn[:, t, s, :], psum("rstd", t)[:, s * TP:s * TP + TP], ln_w[:, s:s + 1],
                                                  qkc[:, t, s, :], ALU.mult, ALU.mult)
                last.then_inc(free("rstd", t), 1)

            def smax(img, h):
                dve.wait_ge(*made(img, "smax", h))
                V.tensor_reduce(max2[:, :, h], psum("smax", h)[0:TC, 0:2 * T].rearrange("p (a b) -> p a b", a=2),
                                op=ALU.max, axis=AX.X).then_inc(free("smax", h), 1)

            def gT_(img, _):
                dve.wait_ge(*made(img, "gT", 0))
                V.tensor_copy(gT[:], psum("gT", 0)[:, 0:TP]).then_inc(free("gT", 0), 1)

            def gn_(img, _):
                dve.wait_ge(*made(img, "sum", 0))
                V.reciprocal(rsum2[:], psum("sum", 0)[:, 0:T]).then_inc(free("sum", 0), 1)
                dve.wait_ge(*read_out(img, "sum", 0))
                dve.wait_ge(*read_out(img, "gT", 0))
                step_c(V.scalar_tensor_tensor(gn[:], gT[:, 0:T], GN_SCALE, rsum2[:], ALU.mult, ALU.mult), img)
                step_c(V.tensor_copy(gn_h[:], gn[:]), img)
                V.tensor_tensor(gn_l[:], gn[:], gn_h[:], op=ALU.subtract).then_inc(s_gn.up(), 1)

            def gh(img, t):
                dve.wait_ge(*made(img, "gh", t))
                dve.wait_ge(*read_out(img, "o2", t))
                V.tensor_tensor(oS[:, t, 0:T], psum("gh", t)[:, 0:T], oT[:, t, :], op=ALU.mult).then_inc(free("gh", t), 1)

            def proj(img, _):
                dve.wait_ge(*made(img, "proj", 0))
                dve.wait_ge(*s_h2b.at(img, 1))
                dve.wait_ge(*s_out.at(img, 0))
                V.tensor_tensor(res[:].rearrange("p a b -> p (a b)"), psum("proj", 0)[0:TC, 0:2 * D],
                                h2b[:].rearrange("p a b -> p (a b)"), op=ALU.add).then_inc(free("proj", 0), 1)

            run_phases(dve, {"fold": fold, "tok": tok, "nx1": nx1, "nx2": nx2, "x1T": x1T_, "q1": q1, "v1": v1_, "s1": s1, "ctx": ctx_, "wo": wo, "x2T": x2T_, "gl": gl,
                             "gate": gate, "v2": v2_, "var": var_, "rstd": rstd_, "lo": low_parts, "smax": smax, "gT": gT_,
                             "gn": gn_, "gh": gh, "proj": proj})

        for name, s in signals.items():
            times = {"x_loaded": 4, "stored": 4}.get(name, 4)
            assert s.made == times * s.per, (name, s.made, s.per)


def laid_out(x, L0_tok_freq_weight_h, L0_tok_freq_weight_w, L0_tok_proj_w, L0_tok_proj_b, L0_tok_cls_token,
             L0_tok_pos_emb, L0_attn_Wq, L0_attn_bq, L0_attn_Wk, L0_attn_bk, L0_attn_Wv, L0_attn_bv, L0_attn_Wo,
             L0_attn_bo, L0_ffn_qkv_w, L0_ffn_qkv_b, L0_ffn_q_norm_w, L0_ffn_q_norm_b, L0_ffn_k_norm_w,
             L0_ffn_k_norm_b, L0_ffn_wg_w, L0_ffn_wg0_w, L0_ffn_wg1_w, L0_ffn_proj_w, L0_ffn_proj_b):
    n = x.shape[0]
    first, mirror = fold_pairs()
    a = {}
    px = np.asarray(x).reshape(n, CH, SIDE, PATCH, SIDE, PATCH).transpose(0, 1, 3, 5, 2, 4).reshape(n, CH, PATCH * PATCH, NPATCH)
    for name, index in (("xa", first), ("xb", mirror)):
        rows = np.zeros((n, KC * KR, NPATCH), np.float32)
        rows[:, :CH * len(index)] = px[:, :, index].reshape(n, -1, NPATCH)
        a[name] = rows.reshape(n, KC, KR, NPATCH).transpose(0, 2, 1, 3)

    def chunked(row):
        return np.broadcast_to(np.asarray(row).reshape(-1), (TC, row.size))

    def kchunks(w, rows):
        w = np.asarray(w)
        return w.reshape(w.shape[0] // rows, rows, -1).transpose(1, 0, 2)

    a["proj_tok"] = np.asarray(L0_tok_proj_w).reshape(D, CH, 2, 72).transpose(3, 2, 1, 0)
    a["freq_h"] = np.repeat(L0_tok_freq_weight_h, PW).reshape(2, 72).T
    a["freq_w"] = np.tile(L0_tok_freq_weight_w, PATCH).reshape(2, 72).T
    pos = np.zeros((TP, D), np.float32)
    pos[:T] = L0_tok_pos_emb[0]
    add = np.zeros((TP, D), np.float32)
    add[0] = np.asarray(L0_tok_cls_token).reshape(-1)
    add[1:T] = L0_tok_proj_b
    a["pos"] = pos.reshape(2, TC, D).transpose(1, 0, 2)
    a["tok_add"] = add.reshape(2, TC, D).transpose(1, 0, 2)
    for name, w in (("wq1", L0_attn_Wq), ("wk1", L0_attn_Wk), ("wv1", L0_attn_Wv)):
        a[name] = kchunks(np.asarray(w).transpose(1, 0, 2).reshape(D, D), DK)
    a["bq1"] = np.asarray(L0_attn_bq).reshape(2, DK).T
    a["bk1"] = np.asarray(L0_attn_bk).reshape(2, DK).T
    a["bv1"] = chunked(L0_attn_bv)
    wo = np.zeros((3, GROUP, 32, D), np.float32)
    wo[:, :, :E1] = np.asarray(L0_attn_Wo).reshape(3, GROUP, E1, D)
    a["wo1"] = wo.reshape(3, 128, D).transpose(1, 0, 2)
    a["bo1"] = chunked(L0_attn_bo)
    a["wgate"] = kchunks(np.concatenate([L0_ffn_wg_w, L0_ffn_wg1_w, L0_ffn_wg0_w], axis=1), DK)
    qkv, qkv_b = np.asarray(L0_ffn_qkv_w), np.asarray(L0_ffn_qkv_b)
    a["wqk"] = kchunks(qkv[:, :2 * H * E2], DK).reshape(DK, 2, 2 * H, E2)
    a["bqk"] = qkv_b[:2 * H * E2].reshape(2, 6, 128).transpose(2, 0, 1)
    a["wv2"] = kchunks(qkv[:, 2 * H * E2:], DK)
    a["bv2"] = chunked(qkv_b[2 * H * E2:])
    a["ln_w"] = np.stack([np.tile(L0_ffn_q_norm_w, 2), np.tile(L0_ffn_k_norm_w, 2)], axis=1)
    a["ln_b"] = np.stack([np.tile(L0_ffn_q_norm_b, 2), np.tile(L0_ffn_k_norm_b, 2)], axis=1)
    a["wp2"] = kchunks(L0_ffn_proj_w, 128)
    a["bp2"] = chunked(L0_ffn_proj_b)
    a.update(shape_constants())
    return {k: np.ascontiguousarray(v) for k, v in a.items()}


def kernel(**inputs):
    import concourse.bacc as bacc
    from concourse.bass_utils import run_bass_kernel_spmd

    nc = bacc.Bacc("TRN2", target_bir_lowering=False, num_devices=1)
    arrays = laid_out(**inputs)
    images = inputs["x"].shape[0]
    ins = {k: nc.dram_tensor(f"in_{k}", v.shape, mybir.dt.from_np(v.dtype), kind="ExternalInput").ap() for k, v in arrays.items()}
    out = nc.dram_tensor("out_tokens", (images, T, D), F32, kind="ExternalOutput").ap()
    build_vit_block(nc, ins, out, images)
    r = run_bass_kernel_spmd(nc, [{f"in_{k}": v for k, v in arrays.items()}], core_ids=[0])
    return r.results[0]["out_tokens"]
```

```python
from contextlib import ExitStack

import numpy as np

import concourse.bass as bass
from concourse import mybir

F32 = mybir.dt.float32
I32 = mybir.dt.int32
F16 = mybir.dt.float16
ALU = mybir.AluOpType
ACT = mybir.ActivationFunctionType
AX = mybir.AxisListType

PATCH, SIDE, CH = 16, 14, 3
NPATCH = SIDE * SIDE
PW = PATCH // 2 + 1
T = NPATCH + 1
TC = 99
TP = 2 * TC
D = 192
DK = 96
DB = DK + 1
H = 12
E1 = 16
E2 = 64
KC, KR = 4, 98
LN_EPS = 1e-5
GATE_EPS = float(np.finfo(np.float32).eps)
NG = 14
RSQRT_GUESS = float(0x5F3759DF)
W_SCALE = 256.0
PREPARED = 1
GROUP = 4
QKN_SLOTS = 3
SLOTS = 6


def fold_pairs():
    first, mirror = [], []
    for h in range(PATCH):
        for w in range(PATCH):
            m = ((-h) % PATCH) * PATCH + (-w) % PATCH
            if h * PATCH + w <= m:
                first.append(h * PATCH + w)
                mirror.append(m)
    return np.array(first), np.array(mirror)


def fold_basis():
    first, mirror = fold_pairs()
    n = len(first)
    u, v = np.divmod(np.arange(PATCH * PW), PW)
    h, w = np.divmod(first, PATCH)
    cos = np.cos(2 * np.pi * ((u[:, None] * h + v[:, None] * w) % PATCH) / PATCH) / PATCH
    cos[:, first == mirror] /= 2
    out = np.zeros((PATCH * PW, CH, KC * KR), np.float32)
    for c in range(CH):
        out[:, c, c * n:(c + 1) * n] = cos
    return np.ascontiguousarray(out.reshape(2, 72, CH, KC * KR).transpose(1, 0, 2, 3))


def shape_constants():
    c = {}
    c["ident"] = np.eye(128, dtype=np.float32)
    sel_var = np.zeros((128, H, 32), np.float32)
    sel_rstd = np.zeros((128, H, 128), np.float32)
    for u in range(H):
        for j in range(2):
            row = 2 * (u // 4) + j
            sel_var[64 * j:64 * j + 64, u, row] = 1.0 / E2
            sel_rstd[32 * (u % 4) + row, u, 64 * j:64 * j + 64] = 1.0
    c["sel_var"], c["sel_rstd"] = sel_var, sel_rstd
    mask = np.zeros((2, GROUP, E1, GROUP), np.float32)
    for j in range(GROUP):
        mask[:, j, :, j] = E1 ** -0.5
    c["mask1"] = mask.reshape(128, GROUP)
    c["iota"] = np.ascontiguousarray(np.broadcast_to(np.arange(10, dtype=np.float32), (TC, 2, 10)))
    c["basis"] = fold_basis()
    return c


class Signal:

    def __init__(self, sem, per):
        self.sem, self.per, self.made = sem, per, 0

    def at(self, img, k):
        assert 0 <= k <= self.per
        return self.sem, img * self.per + k

    def up(self, n=1):
        self.made += n
        return self.sem


class Bank:

    def __init__(self, tensor, full, free):
        self.tensor, self.full, self.free = tensor, full, free


BANKS = {"tok": (2,), "x1T": (2,), "qk1": (0, 1), "v1": (2,), "s1": (0, 1), "ctx": (2,), "wo": (2,), "x2T": (2,),
         "gl": (6,), "qk": (6,), "v2": (6,), "var": (7,),
         "rstd": (3, 4, 5), "s2": (3, 4, 5), "pT": (3, 4, 5), "o2": (3, 4, 5), "proj": (3, 4, 5)}

ORDER = """
C:rstd0 A:fold C:rstd1 C:rstd2 B:qk0 C:kp0 C:kp1 C:lo0 C:kp2 C:lo1 C:rstd3 A:tok B:qk1 C:s2_0 C:s2_1 A:nx1 C:s2_2 B:gl
C:kp3 C:s2_3 B:sq0 C:lo2 C:gr0 C:gr1 A:x1T C:sc0 C:sc1 B:sq1 B:qk2 C:s2_4 C:s2_5 C:rstd4 B:gate0 C:lo3 C:gr2 A:qk1_0
C:lo4 B:gate1 A:qk1_1 C:pT_0 C:sc2 B:qk3 C:pT_1 C:pT_2 A:qk1_2 C:pT_3 C:pT_4 C:s2_6 C:rstd5 C:s2_7 C:kp4 B:qk4 B:ms0
C:pT_5 A:km C:s2_8 C:kp5 B:sq2 A:s1_0 A:s1_1 B:ms1 C:gr3 C:o2_0 C:s2_9 C:lo5 C:o2_1 A:s1_2 B:sq3 A:s1_3 C:sc3 A:v1
B:ms2 B:gate2 C:pT_6 A:s1_4 B:qk5 B:sq4 A:s1_5 C:s2_10 C:s2_11 C:gr4 A:s1_6 B:ms3 C:pT_7 A:s1_7 B:ms4 C:o2_2 B:sq5
B:ms5 A:ctx0 C:sc4 C:gr5 C:sc5 C:h2c C:pT_8 B:var0 B:var1 C:pT_9 A:s1_8 A:s1_9 C:o2_3 C:pT_10 C:pT_11 A:ctx1 B:var2
A:s1_10 A:s1_11 C:o2_4 C:o2_5 B:v2_0 A:ctx2 B:h2b B:gate3 B:var3 B:v2_1 A:wo B:var4 B:v2_2 A:nx2 C:proj B:v2_3 A:x2T
""".split()


def steps_of(phases):
    for entry in ORDER:
        phase, step = entry.split(":")
        if phase in phases:
            name = step.rstrip("0123456789").rstrip("_")
            if step in ("x1T", "x2T", "v1", "nx1", "nx2", "h2b", "h2c"):
                name = step
            elif step.startswith(("qk1_", "s1_", "s2_", "v2_", "o2_", "pT_")):
                    name = step.split("_")[0]
            number = step[len(name):].lstrip("_")
            yield phase, name, int(number) if number else 0


def bank_uses():
    uses, count, turn = {}, [0] * 8, {}
    for _, name, n in [step for phase in "ABC" for step in steps_of(phase)]:
        if name not in BANKS or (name == "var" and n > 0):
            continue
        ring = BANKS[name]
        b = ring[turn.get(ring, 0) % len(ring)]
        turn[ring] = turn.get(ring, 0) + 1
        uses[name, n] = (b, count[b])
        count[b] += 1
    return uses, count


def build_vit_block(nc, ins, out, images):
    with ExitStack() as ctx:
        def sb(name, shape, dt=F32):
            return ctx.enter_context(nc.sbuf_tensor(name, shape, dt))

        signals = {}

        def signal(name, per):
            signals[name] = Signal(ctx.enter_context(nc.semaphore(name)), per)
            return signals[name]

        p1 = sb("p1", [128, H, 2, T])
        pT = sb("pT", [128, H, 2, T])
        room = [p[0:DB].rearrange("p h c t -> p (h c t)") for p in (p1, pT)]
        taken = [0, 0]

        def raw(which, rows, *dims):
            n = int(np.prod(dims))
            ap = room[which][0:rows, taken[which]:taken[which] + n]
            taken[which] += n
            assert taken[which] <= 2 * H * T
            names = "abcd"[:len(dims)]
            return ap.rearrange(f"p ({' '.join(names)}) -> p {' '.join(names)}", **dict(zip(names, dims)))

        basis = raw(1, 72, 2, CH, KC * KR)
        wqk = raw(0, DB, 2, 2 * H, E2)
        wv2_raw = raw(1, DB, 2, H * E2)
        wqk1_raw = sb("wqk1_raw", [DB, 2, 2 * 3 * 128])
        wv1_raw = raw(0, DB, 2, D)
        wgate_raw = raw(0, DB, 2, NG)
        proj_tok = sb("proj_tok", [72, 2, CH, D])
        sel_rstd_raw = sb("sel_rstd_raw", [128, H, 128])
        ident = sb("ident", [128, 128])
        sel_var = sb("sel_var", [128, H, 32])
        sel_rstd = sb("sel_rstd", [128, H, 128], F16)
        mask1 = sb("mask1", [128, GROUP])
        iota = sb("iota", [TC, 2, 10])
        freq_h = sb("freq_h", [72, 2])
        freq_w = sb("freq_w", [72, 2])
        weff = sb("weff", [KR, KC, D])
        pos = sb("pos", [TC, 2, D])
        tok_add = sb("tok_add", [TC, 2, D])
        posb = sb("posb", [TC, 2, D])
        wqk1 = [sb(f"wqk1_{x}", [DB, 2, 2 * 3 * 128], F16) for x in "hl"]
        wv1 = [sb(f"wv1_{x}", [DB, 2, D], F16) for x in "hl"]
        wgate = [sb(f"wgate_{x}", [DB, 2, NG], F16) for x in "hl"]
        wqkc = [sb(f"wqkc_{x}", [DB, 2, 2 * H, E2], F16) for x in "hl"]
        wv2 = [sb(f"wv2_{x}", [DB, 2, H * E2], F16) for x in "hl"]
        wo1 = sb("wo1", [128, 3, D])
        bo1 = sb("bo1", [TC, D])
        wqk_mean = sb("wqk_mean", [DB, 2, 2 * H])
        ln_w = sb("ln_w", [128, 2])
        ln_b = sb("ln_b", [128, 2])
        wp2 = sb("wp2", [128, 6, D])
        bp2 = sb("bp2", [TC, D])
        mhalf = sb("mhalf", [TC, 2])
        ones = sb("ones", [TC, 2])

        xa = sb("xa", [KR, KC, NPATCH])
        xb = sb("xb", [KR, KC, NPATCH])
        xs = sb("xs", [KR, KC, TP])
        h1 = sb("h1", [TC, 2, D])
        h1b = sb("h1b", [TC, 2, D])
        stats = sb("stats", [TC, 2, 6])
        both = sb("both", [TC, 2, 2])
        apart = sb("apart", [TC, 2])
        mean = sb("mean", [TC, 2])
        vare = sb("vare", [TC, 2])
        rstd = sb("rstd", [TC, 2])
        x1 = sb("x1", [TC, 2, D])
        x1T = [sb(f"x1T_{x}", [DB, 2, TP], F16) for x in "hl"]
        qk1 = sb("qk1", [128, 3, 3, TP], F16)
        km1 = sb("km1", [128, H, TP], F16)
        v1 = sb("v1", [TC, 2, D])
        nmax1 = sb("nmax1", [TC, 2, H])
        sum1 = sb("sum1", [TC, 2, H])
        rsum1 = sb("rsum1", [TC, 2, H])
        vs1 = sb("vs1", [128, 2, H, 32])
        ctxT = sb("ctxT", [128, 3, TP])
        h2 = sb("h2", [TC, 2, D])
        x2 = x1
        x2T = [sb(f"x2T_{x}", [DB, 2, TP], F16) for x in "hl"]
        h2b = sb("h2b", [TC, 2, D])
        h2c = sb("h2c", [TC, 2, D])
        glog = sb("glog", [TC, 2, NG])
        gexp = sb("gexp", [TC, 2, NG])
        gsm = sb("gsm", [TC, 2, NG])
        gtmp = sb("gtmp", [TC, 6, 2, 10])
        gred = sb("gred", [TC, 12, 2, 2])
        mg = sb("mg", [TC, H, 2])
        qkc = sb("qkc", [128, 6, 2, TP])
        sq = sb("sq", [128, 6, 2, TP])
        qkn = sb("qkn", [128, QKN_SLOTS, 2, TP])
        var = sb("var", [128, TP])
        rs = sb("rs", [128, TP])
        rs_h = sb("rs_h", [128, TP], F16)
        rs_l = sb("rs_l", [128, TP], F16)
        newton = sb("newton", [128, TP])
        qh = sb("qh", [128, H, TP], F16)
        ql = sb("ql", [128, H, TP], F16)
        kh = sb("kh", [128, 6, TP], F16)
        kl = sb("kl", [128, 6, TP], F16)
        v2 = sb("v2", [128, 2, H * E2])
        nmax2 = sb("nmax2", [TC, H, 2])
        sum2 = sb("sum2", [TC, H, 2])
        rsum2 = sb("rsum2", [TC, H, 2])
        gn = sb("gn", [TC, H, 2])
        pq = sb("pq", [TC, SLOTS, 2, TP])
        oT = sb("oT", [128, 6, TP])
        res = sb("res", [TC, 2, D])

        uses, count = bank_uses()
        banks = [Bank(ctx.enter_context(nc.psum_tensor(f"bank{b}", [128, 512], F32)),
                      signal(f"bank{b}_full", count[b]), signal(f"bank{b}_free", count[b])) for b in range(len(count))]

        def psum(*key):
            return banks[uses[key][0]].tensor

        def room_for(img, *key):
            b, n = uses[key]
            return banks[b].free.at(img, n)

        def free_before(img, name):
            b, n = uses[name, 0]
            return banks[b].free.at(img, 0)

        def made(img, *key):
            b, n = uses[key]
            return banks[b].full.at(img, n + 1)

        def read_out(img, *key):
            b, n = uses[key]
            return banks[b].free.at(img, n + 1)

        def lasts(name, numbers):
            last = {uses[name, n][0]: n for n in numbers}
            return sorted(last.values())

        def full(*key):
            return banks[uses[key][0]].full.up()

        def free(*key):
            return banks[uses[key][0]].free.up()

        s_load = signal("x_loaded", 32)
        s_fold = signal("xs_folded", 1)
        s_mv = signal("mean_var_ready", 2)
        s_rstd = signal("rstd_ready", 2)
        s_x1 = signal("x1_ready", 1)
        s_h1b = signal("h1_bias_ready", 1)
        s_qkh = signal("qk1_high_parts", 3)
        s_km = signal("k1_masked", 1)
        s_x1h = signal("x1T_high_ready", 1)
        s_nm = signal("max1_ready", H)
        s_vs = signal("v1_scaled", 3)
        s_x2 = signal("x2_ready", 1)
        s_x2h = signal("x2T_high_ready", 1)
        s_h2b = signal("h2_bias_ready", 1)
        s_h2c = signal("h2_bias_kept", 1)
        s_gmax = signal("gate_logits_shifted", 1)
        s_gexp = signal("gate_exp_ready", 1)
        s_gate = signal("gates_ready", 1)
        s_sq = signal("qk_squared", 6)
        s_rs = signal("head_rstd_ready", 1)
        s_hi = signal("q_high_parts", 6)
        s_lo = signal("q_low_parts", 6)
        s_kb = signal("k_with_bias", 6)
        s_kh = signal("k_high_parts", 6)
        s_kl = signal("k_low_parts", 6)
        s_nm2 = signal("max2_ready", H)
        s_rsum2 = signal("sum2_inverted", 6)
        s_gn = signal("gate_over_sum_ready", 6)
        s_sc = signal("probs2_scaled", 6)
        s_out = signal("stored", 32)
        s_step_a = signal("vector_step_a", 9)
        s_step_b = signal("vector_step_b", 34)
        s_w = ctx.enter_context(nc.semaphore("weights_loaded"))
        s_const = ctx.enter_context(nc.semaphore("weights_prepared"))
        s_pool = ctx.enter_context(nc.semaphore("padding_zeroed"))
        s_prep = ctx.enter_context(nc.semaphore("prep_vector_step"))
        s_pw = ctx.enter_context(nc.semaphore("token_weights_scaled"))
        s_weff = ctx.enter_context(nc.semaphore("token_weights_in_psum"))

        block = ctx.enter_context(nc.Block())

        loads = [(basis, "basis"), (proj_tok[:], "proj_tok"), (freq_h[:], "freq_h"), (freq_w[:], "freq_w"),
                 (wqk, "wqk"), (wqk1_raw[:], "wqk1"), (wv1_raw, "wv1"), (wgate_raw, "wgate"), (wv2_raw, "wv2"), (sel_rstd_raw[:], "sel_rstd"),
                 (ident[:], "ident"),
                 (sel_var[:], "sel_var"), (mask1[:], "mask1"), (iota[:], "iota"),
                 (pos[:], "pos"), (tok_add[:], "tok_add"), 
                 (wo1[:], "wo1"), (bo1[:], "bo1"), (ln_w[:], "ln_w"), (ln_b[:], "ln_b"),
                 (wp2[:], "wp2"), (bp2[:], "bp2")]

        def run_phases(eng, steps):
            def go(phases, image):
                for phase, name, n in steps_of(phases):
                    if name in steps:
                        steps[name](image[phase], n)

            go("A", {"A": 0})
            go("AB", {"A": 1, "B": 0})
            go("ABC", {"A": 2, "B": 1, "C": 0})
            with eng.Fori(1, images - 2) as i:
                go("ABC", {"A": i + 2, "B": i + 1, "C": i})
            go("BC", {"B": images - 1, "C": images - 2})
            go("C", {"C": images - 1})

        @block.sync
        def _(sp):
            for dst, name in loads:
                sp.dma_start(dst, ins[name]).then_inc(s_w, 16)

            def load(img):
                sp.wait_ge(*s_fold.at(img, 0))
                sp.dma_start(xa[:], ins["xa"][bass.ds(img, 1)].rearrange("b p k n -> (b p) k n")).then_inc(s_load.up(16), 16)
                sp.dma_start(xb[:], ins["xb"][bass.ds(img, 1)].rearrange("b p k n -> (b p) k n")).then_inc(s_load.up(16), 16)

            def store(img):
                sp.wait_ge(*read_out(img, "proj", 0))
                dst = out[bass.ds(img, 1)].rearrange("b t d -> (b t) d")
                sp.dma_start(dst[0:TC, :], res[:, 0, :]).then_inc(s_out.up(16), 16)
                sp.dma_start(dst[TC:T, :], res[0:T - TC, 1, :]).then_inc(s_out.up(16), 16)

            for img in range(4):
                load(img)
            store(0)
            with sp.Fori(1, images - 3) as i:
                load(i + 3)
                store(i)
            for img in range(images - 3, images):
                store(img)
            sp.wait_ge(s_out.sem, s_out.per * images)

        @block.gpsimd
        def _(pool):
            pool.wait_ge(s_const, PREPARED)
            nc.gpsimd.memset(p1[96:128], 0.0).then_inc(s_pool, 1)
            nc.gpsimd.memset(pT[96:128], 0.0).then_inc(s_pool, 1)

            def inverse_root(img, layer):
                pool.wait_ge(*s_mv.at(img, layer + 1))
                nc.gpsimd.tensor_tensor(rstd[:], vare[:], mhalf[:], op=ALU.pow).then_inc(s_rstd.up(), 1)

            def tok(img, _):
                inverse_root(img, 0)
                pool.wait_ge(*read_out(img, "tok", 0))
                for c in range(2):
                    last = nc.gpsimd.tensor_tensor(h1b[:, c, :], h1[:, c, :], bo1[:], op=ALU.add)
                last.then_inc(s_h1b.up(), 1)

            def wo(img, _):
                inverse_root(img, 1)

            def h2b_(img, _):
                pool.wait_ge(*read_out(img, "wo", 0))
                pool.wait_ge(*s_h2c.at(img, 0))
                for c in range(2):
                    last = nc.gpsimd.tensor_tensor(h2b[:, c, :], h2[:, c, :], bp2[:], op=ALU.add)
                last.then_inc(s_h2b.up(), 1)

            def h2c_(img, _):
                pool.wait_ge(*s_h2b.at(img, 1))
                pool.wait_ge(*free_before(img, "proj"))
                nc.gpsimd.tensor_tensor(h2c[:], h2b[:], ones[:].unsqueeze(2).to_broadcast([TC, 2, D]), op=ALU.mult).then_inc(s_h2c.up(), 1)

            def scale(img, t):
                pool.wait_ge(*s_gn.at(img, t + 1))
                pair = pq[:, 2 * t % SLOTS:2 * t % SLOTS + 2].rearrange("p h c t -> p (h c) t")[:, :, 0:T]
                factor = gn[:, 2 * t:2 * t + 2, :].rearrange("p h c -> p (h c)").unsqueeze(2).to_broadcast([TC, 4, T])
                nc.gpsimd.tensor_tensor(pair, pair, factor, op=ALU.mult).then_inc(s_sc.up(), 1)

            def square(img, t):
                pool.wait_ge(*read_out(img, "qk", t))
                nc.gpsimd.tensor_tensor(sq[:, t], qkc[:, t], qkc[:, t], op=ALU.mult).then_inc(s_sq.up(), 1)

            def k_parts(img, t):
                k = qkn[:, t % QKN_SLOTS, 1, :]
                pool.wait_ge(*read_out(img, "rstd", t))
                nc.gpsimd.tensor_tensor(kh[:, t, :], k, ln_b[:, 1:2].to_broadcast([128, TP]), op=ALU.add).then_inc(s_kh.up(), 1)
                pool.wait_ge(*s_kh.at(img, t + 1))
                nc.gpsimd.tensor_tensor(k, k, ln_b[:, 1:2].to_broadcast([128, TP]), op=ALU.add).then_inc(s_kb.up(), 1)
                pool.wait_ge(*s_kb.at(img, t + 1))
                nc.gpsimd.tensor_tensor(kl[:, t, :], k, kh[:, t, :], op=ALU.subtract).then_inc(s_kl.up(), 1)

            run_phases(pool, {"sq": square, "kp": k_parts, "tok": tok, "wo": wo, "h2b": h2b_, "h2c": h2c_, "sc": scale})

        @block.tensor
        def _(pe):
            def mm(o, l, r, first=True, last=True):
                return nc.tensor.matmul(o, l, r, start=first, stop=last)

            def mm3(o, l, r, first=True, last=True):
                mm(o, l[0], r[0], first, False)
                mm(o, l[1], r[0], False, False)
                return mm(o, l[0], r[1], False, last)

            pe.wait_ge(s_w, 16 * len(loads))
            pe.wait_ge(s_pw, 1)
            for k in range(KC):
                for n in range(6):
                    c, a = divmod(n, 2)
                    mm(banks[k].tensor[0:KR, 0:D], basis[:, a, c, KR * k:KR * k + KR], proj_tok[:, a, c, :], n == 0, n == 5).then_inc(s_weff, 1)
            pe.wait_ge(s_const, PREPARED)
            pe.wait_ge(s_pool, 2)

            def tok(img, _):
                o = psum("tok", 0)
                pe.wait_ge(*room_for(img, "tok", 0))
                pe.wait_ge(*s_fold.at(img, 1))
                for c in range(2):
                    for k in range(KC):
                        last = mm(o[0:TC, c * D:c * D + D], xs[:, k, c * TC:c * TC + TC], weff[:, k, :], k == 0, k == KC - 1)
                last.then_inc(full("tok", 0), 1)

            def transposes(o, src):
                for kc in range(2):
                    for c in range(2):
                        last = nc.tensor.transpose(o[0:DK, kc * TP + c * TC:kc * TP + c * TC + TC],
                                                   src[:, c, kc * DK:kc * DK + DK], ident[0:TC, 0:TC])
                return last

            def x1T_(img, _):
                pe.wait_ge(*room_for(img, "x1T", 0))
                pe.wait_ge(*s_x1.at(img, 1))
                transposes(psum("x1T", 0), x1).then_inc(full("x1T", 0), 1)

            def x2T_(img, _):
                pe.wait_ge(*room_for(img, "x2T", 0))
                pe.wait_ge(*s_x2.at(img, 1))
                transposes(psum("x2T", 0), x2).then_inc(full("x2T", 0), 1)

            def qk1_(img, g):
                o = psum("qk1", g)
                pe.wait_ge(*room_for(img, "qk1", g))
                if g == 0:
                    pe.wait_ge(*read_out(img, "x1T", 0))
                for s in range(2):
                    w = slice(128 * (3 * s + g), 128 * (3 * s + g) + 128)
                    for kc in range(2):
                        last = mm3(o[:, s * TP:s * TP + TP], [x[:, kc, w] for x in wqk1], [x[:, kc, :] for x in x1T], kc == 0, kc == 1)
                last.then_inc(full("qk1", g), 1)

            def v1_(img, _):
                o = psum("v1", 0)
                pe.wait_ge(*room_for(img, "v1", 0))
                pe.wait_ge(*read_out(img, "x1T", 0))
                for c in range(2):
                    for kc in range(2):
                        last = mm3(o[0:TC, c * D:c * D + D], [x[:, kc, c * TC:c * TC + TC] for x in x1T],
                                   [x[:, kc, :] for x in wv1], kc == 0, kc == 1)
                last.then_inc(full("v1", 0), 1)

            def s1(img, h):
                o = psum("s1", h)
                pe.wait_ge(*room_for(img, "s1", h))
                if h == 0:
                    pe.wait_ge(*s_km.at(img, 1))
                for c in range(2):
                    for part in (0, 2):
                        last = mm(o[0:TC, c * T:c * T + T], km1[:, h, c * TC:c * TC + TC], qk1[:, h // GROUP, part, 0:T], part == 0, part == 2)
                last.then_inc(full("s1", h), 1)

            def ctx_(img, g):
                o = psum("ctx", g)
                pe.wait_ge(*room_for(img, "ctx", g))
                pe.wait_ge(*s_vs.at(img, g + 1))
                for h in lasts("s1", range(GROUP * g, GROUP * g + GROUP)):
                    pe.wait_ge(*read_out(img, "s1", h))
                for c in range(2):
                    for j in range(GROUP):
                        h = GROUP * g + j
                        last = mm(o[32 * j:32 * j + 32, 0:T], vs1[:, c, h, :], p1[:, h, c, :], c == 0, c == 1)
                last.then_inc(full("ctx", g), 1)

            def wo(img, _):
                o = psum("wo", 0)
                pe.wait_ge(*room_for(img, "wo", 0))
                pe.wait_ge(*read_out(img, "ctx", 2))
                for c in range(2):
                    for g in range(3):
                        last = mm(o[0:TC, c * D:c * D + D], ctxT[:, g, c * TC:c * TC + TC], wo1[:, g, :], g == 0, g == 2)
                last.then_inc(full("wo", 0), 1)

            def gl(img, _):
                o = psum("gl", 0)
                pe.wait_ge(*room_for(img, "gl", 0))
                pe.wait_ge(*read_out(img, "x2T", 0))
                for c in range(2):
                    for kc in range(2):
                        last = mm3(o[0:TC, c * NG:c * NG + NG], [x[:, kc, c * TC:c * TC + TC] for x in x2T],
                                   [x[:, kc, :] for x in wgate], kc == 0, kc == 1)
                last.then_inc(full("gl", 0), 1)

            def mean_square(img, t):
                if t == 0:
                    pe.wait_ge(*room_for(img, "var", 0))
                pe.wait_ge(*s_sq.at(img, t + 1))
                for s in range(2):
                    u = 2 * t + s
                    q = 32 * (u % 4)
                    last = mm(psum("var", 0)[q:q + 32, 0:TP], sel_var[:, u, :], sq[:, t, s, :], u < 4, u >= 8)
                if t == 5:
                    last.then_inc(full("var", 0), 1)

            def qk(img, t):
                o = psum("qk", t)
                pe.wait_ge(*room_for(img, "qk", t))
                pe.wait_ge(*read_out(img, "x2T", 0))
                for s in range(2):
                    for kc in range(2):
                        w = [x[:, kc, H * s + 2 * t:H * s + 2 * t + 2, :].rearrange("p a b -> p (a b)") for x in wqkc]
                        last = mm3(o[:, s * TP:s * TP + TP], w, [x[:, kc, :] for x in x2T], kc == 0, kc == 1)
                last.then_inc(full("qk", t), 1)

            def v2_(img, n):
                c, a = divmod(n, 2)
                o = psum("v2", n)
                pe.wait_ge(*room_for(img, "v2", n))
                for kc in range(2):
                    last = mm3(o[0:TC, 0:384], [x[:, kc, c * TC:c * TC + TC] for x in x2T],
                               [x[:, kc, 384 * a:384 * a + 384] for x in wv2], kc == 0, kc == 1)
                last.then_inc(full("v2", n), 1)

            def rstd_(img, t):
                o = psum("rstd", t)
                pe.wait_ge(*room_for(img, "rstd", t))
                pe.wait_ge(*s_rs.at(img, 1))
                for s in range(2):
                    mm(o[:, s * TP:s * TP + TP], sel_rstd[:, 2 * t + s, :], rs_h[:], True, False)
                    last = mm(o[:, s * TP:s * TP + TP], sel_rstd[:, 2 * t + s, :], rs_l[:], False, True)
                last.then_inc(full("rstd", t), 1)

            def s2(img, h):
                o = psum("s2", h)
                pe.wait_ge(*room_for(img, "s2", h))
                pe.wait_ge(*s_lo.at(img, h // 2 + 1))
                pe.wait_ge(*s_kl.at(img, h // 2 + 1))
                for c in range(2):
                    cols = slice(c * TC, c * TC + TC)
                    last = mm3(o[0:TC, c * T:c * T + T], (qh[:, h, cols], ql[:, h, cols]), (kh[:, h // 2, 0:T], kl[:, h // 2, 0:T]))
                last.then_inc(full("s2", h), 1)

            def pT_(img, h):
                o = psum("pT", h)
                pe.wait_ge(*room_for(img, "pT", h))
                pe.wait_ge(*s_sc.at(img, h // 2 + 1))
                for k in range(2):
                    for c in range(2):
                        n = TC - c
                        last = nc.tensor.transpose(o[0:TC, k * T + c * TC:k * T + c * TC + n],
                                                   pq[0:n, h % SLOTS, c, k * TC:k * TC + TC], ident[0:n, 0:n])
                last.then_inc(full("pT", h), 1)

            def o2(img, t):
                o = psum("o2", t)
                pe.wait_ge(*room_for(img, "o2", t))
                if t == 0:
                    pe.wait_ge(*read_out(img, "v2", 3))
                for h in lasts("pT", (2 * t, 2 * t + 1)):
                    pe.wait_ge(*read_out(img, "pT", h))
                for c in range(2):
                    for j in range(2):
                        h = 2 * t + j
                        last = mm(o[64 * j:64 * j + 64, 0:T], v2[:, c, E2 * h:E2 * h + E2], pT[:, h, c, :], c == 0, c == 1)
                last.then_inc(full("o2", t), 1)

            def proj(img, _):
                o = psum("proj", 0)
                pe.wait_ge(*room_for(img, "proj", 0))
                pe.wait_ge(*read_out(img, "o2", 5))
                for c in range(2):
                    for t in range(6):
                        last = mm(o[0:TC, c * D:c * D + D], oT[:, t, c * TC:c * TC + TC], wp2[:, t, :], t == 0, t == 5)
                last.then_inc(full("proj", 0), 1)

            run_phases(pe, {"tok": tok, "x1T": x1T_, "qk1": qk1_, "v1": v1_, "s1": s1, "ctx": ctx_, "wo": wo, "x2T": x2T_, "gl": gl,
                            "qk": qk, "ms": mean_square, "v2": v2_, "rstd": rstd_, "s2": s2, "pT": pT_, "o2": o2, "proj": proj})

        @block.scalar
        def _(act):
            act.wait_ge(s_const, PREPARED)
            act.wait_ge(s_pool, 2)

            def x1T_(img, _):
                act.wait_ge(*made(img, "x1T", 0))
                nc.scalar.activation(x1T[0][0:DK].rearrange("p a b -> p (a b)"), psum("x1T", 0)[0:DK, 0:2 * TP],
                                     ACT.Copy).then_inc(s_x1h.up(), 1)

            def x2T_(img, _):
                act.wait_ge(*made(img, "x2T", 0))
                nc.scalar.activation(x2T[0][0:DK].rearrange("p a b -> p (a b)"), psum("x2T", 0)[0:DK, 0:2 * TP],
                                     ACT.Copy).then_inc(s_x2h.up(), 1)

            def qk1_(img, g):
                act.wait_ge(*made(img, "qk1", g))
                nc.scalar.activation(qk1[:, g, 0:2, :].rearrange("p a b -> p (a b)"), psum("qk1", g)[:, 0:2 * TP], ACT.Copy,
                                     scale=1.0 / W_SCALE).then_inc(s_qkh.up(), 1)

            def v1_(img, _):
                act.wait_ge(*made(img, "v1", 0))
                nc.scalar.activation(v1[:].rearrange("p a b -> p (a b)"), psum("v1", 0)[0:TC, 0:2 * D], ACT.Copy,
                                     scale=1.0 / W_SCALE).then_inc(free("v1", 0), 1)

            def s1(img, h):
                act.wait_ge(*made(img, "s1", h))
                act.wait_ge(*s_nm.at(img, h + 1))
                for c in range(2):
                    last = nc.scalar.activation(p1[0:TC, h, c, :], psum("s1", h)[0:TC, c * T:c * T + T], ACT.Exp,
                                                bias=nmax1[:, c, h:h + 1], accum_out=sum1[:, c, h:h + 1])
                last.then_inc(free("s1", h), 1)

            def ctx_(img, g):
                act.wait_ge(*made(img, "ctx", g))
                nc.scalar.activation(ctxT[:, g, 0:T], psum("ctx", g)[:, 0:T], ACT.Copy).then_inc(free("ctx", g), 1)

            def qk(img, t):
                act.wait_ge(*made(img, "qk", t))
                nc.scalar.activation(qkc[:, t].rearrange("p a b -> p (a b)"), psum("qk", t)[:, 0:2 * TP], ACT.Copy,
                                     scale=1.0 / W_SCALE).then_inc(free("qk", t), 1)

            def gate(img, n):
                if n != 1:
                    return
                act.wait_ge(*s_gmax.at(img, 1))
                nc.scalar.activation(gexp[:], glog[:], ACT.Exp).then_inc(s_gexp.up(), 1)

            def rstd_(img, t):
                act.wait_ge(*read_out(img, "rstd", t))
                for j in range(2):
                    r = slice(64 * j, 64 * j + 64)
                    last = nc.scalar.activation(qh[r, 2 * t + j, :], qkn[r, t % QKN_SLOTS, 0, :], ACT.Identity, bias=ln_b[r, 0:1])
                last.then_inc(s_hi.up(), 1)

            def s2(img, h):
                act.wait_ge(*made(img, "s2", h))
                act.wait_ge(*s_nm2.at(img, h + 1))
                for c in range(2):
                    last = nc.scalar.activation(pq[0:TC, h % SLOTS, c, 0:T], psum("s2", h)[0:TC, c * T:c * T + T], ACT.Exp,
                                                bias=nmax2[:, h, c:c + 1], accum_out=sum2[:, h, c:c + 1])
                last.then_inc(free("s2", h), 1)

            def pT_(img, h):
                act.wait_ge(*made(img, "pT", h))
                nc.scalar.activation(pT[0:TC, h].rearrange("p a b -> p (a b)"), psum("pT", h)[0:TC, 0:2 * T],
                                     ACT.Copy).then_inc(free("pT", h), 1)

            def o2(img, t):
                act.wait_ge(*made(img, "o2", t))
                nc.scalar.activation(oT[:, t, 0:T], psum("o2", t)[:, 0:T], ACT.Copy).then_inc(free("o2", t), 1)

            run_phases(act, {"x1T": x1T_, "qk1": qk1_, "v1": v1_, "s1": s1, "ctx": ctx_, "x2T": x2T_, "gate": gate, "qk": qk,
                             "rstd": rstd_, "s2": s2, "pT": pT_, "o2": o2})

        @block.vector
        def _(dve):
            V = nc.vector
            dve.wait_ge(s_w, 16 * len(loads))
            prep = [0]

            def link(ins_):
                prep[0] += 1
                ins_.then_inc(s_prep, 1)
                dve.wait_ge(s_prep, prep[0])

            for a in range(2):
                v = proj_tok[:, a].rearrange("p c d -> p (c d)")
                link(V.tensor_scalar(v, v, freq_h[:, a:a + 1], freq_w[:, a:a + 1], ALU.mult, ALU.mult))
            V.memset(xs[:], 0.0).then_inc(s_pw, 1)
            link(V.tensor_reduce(wqk_mean[:], wqk, op=ALU.add, axis=AX.X))
            link(V.tensor_scalar(wqk_mean[:], wqk_mean[:], 1.0 / E2, None, ALU.mult))
            for kc in range(2):
                link(V.tensor_tensor(wqk[:, kc], wqk[:, kc], wqk_mean[:, kc].unsqueeze(2).to_broadcast([DB, 2 * H, E2]),
                                     op=ALU.subtract))
            for source, parts in ((wqk, wqkc), (wv2_raw, wv2), (wqk1_raw[:], wqk1), (wv1_raw, wv1), (wgate_raw, wgate)):
                whole = "p a b c -> p (a b c)" if len(source.shape) == 4 else "p a b -> p (a b)"
                high, low = (x[:].rearrange(whole) for x in parts)
                source = source.rearrange(whole)
                link(V.tensor_scalar(high, source, W_SCALE, None, ALU.mult))
                link(V.scalar_tensor_tensor(low, source, W_SCALE, high, ALU.mult, ALU.subtract))
            for x in (x1T, x2T):
                link(V.memset(x[0][DK:DB], 1.0))
                link(V.memset(x[1][DK:DB], 0.0))
            link(V.tensor_tensor(posb[:], pos[:], tok_add[:], op=ALU.add))
            link(V.tensor_copy(sel_rstd[:], sel_rstd_raw[:]))
            link(V.tensor_scalar(ln_w[:, 0:1], ln_w[:, 0:1], E2 ** -0.5, None, ALU.mult))
            link(V.tensor_scalar(ln_b[:, 0:1], ln_b[:, 0:1], E2 ** -0.5, None, ALU.mult))
            for x in (mhalf,):
                link(V.memset(x[:], -0.5))
            link(V.memset(ones[:], 1.0))
            for x in (vs1, ctxT, qh, ql, pq, oT, v2):
                link(V.memset(x[:], 0.0))
            dve.wait_ge(s_weff, 6 * KC)
            for k in range(KC):
                link(V.tensor_copy(weff[:, k, :], banks[k].tensor[0:KR, 0:D]))
            V.memset(gtmp[:], 0.0).then_inc(s_const, PREPARED)
            dve.wait_ge(s_const, PREPARED)

            def step_a(ins_, img):
                ins_.then_inc(s_step_a.up(), 1)
                dve.wait_ge(*s_step_a.at(img, (s_step_a.made - 1) % s_step_a.per + 1))

            def step_b(ins_, img):
                ins_.then_inc(s_step_b.up(), 1)
                dve.wait_ge(*s_step_b.at(img, (s_step_b.made - 1) % s_step_b.per + 1))

            def moments(img, src):
                for c in range(2):
                    last = V.bn_stats(stats[:, c, :], src[:, c, :])
                step_a(last, img)
                halves = stats[:].rearrange("p c (o s) -> p c o s", o=2)
                V.tensor_tensor(both[:], halves[:, :, 0, 1:3], halves[:, :, 1, 1:3], op=ALU.add)
                step_a(V.tensor_tensor(apart[:], halves[:, :, 0, 1], halves[:, :, 1, 1], op=ALU.subtract), img)
                V.tensor_scalar(mean[:], both[:, :, 0], 0.5, None, ALU.mult)
                V.tensor_scalar(vare[:], both[:, :, 1], 1.0 / D, LN_EPS, ALU.mult, ALU.add)
                step_a(V.tensor_tensor(apart[:], apart[:], apart[:], op=ALU.mult), img)
                V.scalar_tensor_tensor(vare[:], apart[:], 0.25, vare[:], ALU.mult, ALU.add).then_inc(s_mv.up(), 1)

            def normalise(img, src, dst, sig, n):
                dve.wait_ge(*s_rstd.at(img, n))
                for c in range(2):
                    last = V.tensor_scalar(dst[:, c, :], src[:, c, :], mean[:, c:c + 1], rstd[:, c:c + 1], ALU.subtract, ALU.mult)
                last.then_inc(sig.up(), 1)

            def fold(img, _):
                dve.wait_ge(*s_load.at(img, 32))
                V.tensor_tensor(xs[:, :, 1:T], xa[:], xb[:], op=ALU.add).then_inc(s_fold.up(), 1)

            def tok(img, _):
                dve.wait_ge(*made(img, "tok", 0))
                dve.wait_ge(*s_h1b.at(img, 0))
                V.tensor_tensor(h1[:].rearrange("p a b -> p (a b)"), psum("tok", 0)[0:TC, 0:2 * D],
                                posb[:].rearrange("p a b -> p (a b)"), op=ALU.add).then_inc(free("tok", 0), 1)
                dve.wait_ge(*read_out(img, "tok", 0))
                moments(img, h1)

            def nx1(img, _):
                normalise(img, h1, x1, s_x1, 1)

            def x1T_(img, _):
                dve.wait_ge(*s_x1h.at(img, 1))
                V.tensor_tensor(x1T[1][0:DK].rearrange("p a b -> p (a b)"), psum("x1T", 0)[0:DK, 0:2 * TP],
                                x1T[0][0:DK].rearrange("p a b -> p (a b)"), op=ALU.subtract).then_inc(free("x1T", 0), 1)

            def qk1_(img, g):
                dve.wait_ge(*s_qkh.at(img, g + 1))
                V.scalar_tensor_tensor(qk1[:, g, 2, :], psum("qk1", g)[:, 0:TP], 1.0 / W_SCALE, qk1[:, g, 0, :], ALU.mult, ALU.subtract)
                V.scalar_tensor_tensor(qk1[64:128, g, 1, :], psum("qk1", g)[64:128, TP:2 * TP], 1.0 / W_SCALE, qk1[64:128, g, 1, :],
                                       ALU.mult, ALU.subtract).then_inc(free("qk1", g), 1)

            def km(img, _):
                for g in lasts("qk1", range(3)):
                    dve.wait_ge(*read_out(img, "qk1", g))
                for j in range(GROUP):
                    last = V.tensor_scalar(km1[:].rearrange("p (g j) t -> p g j t", j=GROUP)[:, :, j, :], qk1[:, :, 1, :],
                                           mask1[:, j:j + 1], None, ALU.mult)
                last.then_inc(s_km.up(), 1)

            def s1(img, h):
                dve.wait_ge(*made(img, "s1", h))
                V.tensor_reduce(nmax1[:, :, h], psum("s1", h)[0:TC, 0:2 * T].rearrange("p (a b) -> p a b", a=2),
                                op=ALU.max, axis=AX.X, negate=True).then_inc(s_nm.up(), 1)

            def ctx_(img, g):
                hs = slice(GROUP * g, GROUP * g + GROUP)
                for h in lasts("s1", range(GROUP * g, GROUP * g + GROUP)):
                    dve.wait_ge(*read_out(img, "s1", h))
                step_a(V.reciprocal(rsum1[:, :, hs], sum1[:, :, hs]), img)
                dve.wait_ge(*read_out(img, "v1", 0))
                for c in range(2):
                    n = TC - c
                    last = V.tensor_tensor(vs1[0:n, c, hs, 0:E1],
                                           v1[0:n, c, E1 * GROUP * g:E1 * GROUP * (g + 1)].rearrange("p (h e) -> p h e", h=GROUP),
                                           rsum1[0:n, c, hs].unsqueeze(2).to_broadcast([n, GROUP, E1]), op=ALU.mult)
                last.then_inc(s_vs.up(), 1)

            def wo(img, _):
                dve.wait_ge(*made(img, "wo", 0))
                dve.wait_ge(*s_h1b.at(img, 1))
                dve.wait_ge(*s_h2b.at(img, 0))
                V.tensor_tensor(h2[:].rearrange("p a b -> p (a b)"), psum("wo", 0)[0:TC, 0:2 * D],
                                h1b[:].rearrange("p a b -> p (a b)"), op=ALU.add).then_inc(free("wo", 0), 1)
                dve.wait_ge(*read_out(img, "wo", 0))
                moments(img, h2)

            def nx2(img, _):
                normalise(img, h2, x2, s_x2, 2)

            def x2T_(img, _):
                dve.wait_ge(*s_x2h.at(img, 1))
                V.tensor_tensor(x2T[1][0:DK].rearrange("p a b -> p (a b)"), psum("x2T", 0)[0:DK, 0:2 * TP],
                                x2T[0][0:DK].rearrange("p a b -> p (a b)"), op=ALU.subtract).then_inc(free("x2T", 0), 1)

            def pairs(x):
                return x[:, :, 10:14].rearrange("p c (a b) -> p c a b", b=2)

            routed = gsm[:, :, 0:10]

            def gl(img, _):
                dve.wait_ge(*made(img, "gl", 0))
                V.tensor_scalar(gsm[:].rearrange("p a b -> p (a b)"), psum("gl", 0)[0:TC, 0:2 * NG], 1.0 / W_SCALE, None,
                                ALU.mult).then_inc(free("gl", 0), 1)

            def first_best(img, src, n):
                step_b(V.tensor_reduce(gred[:, 6 + 2 * n, :, 0], src, op=ALU.max, axis=AX.X), img)
                step_b(V.tensor_tensor(gtmp[:, 2 + n], src, gred[:, 6 + 2 * n, :, 0:1].to_broadcast([TC, 2, 10]), op=ALU.is_equal), img)
                step_b(V.scalar_tensor_tensor(gtmp[:, 2 + n], gtmp[:, 2 + n], -100.0, iota[:], ALU.mult, ALU.add), img)
                step_b(V.tensor_reduce(gred[:, 7 + 2 * n, :, 0], gtmp[:, 2 + n], op=ALU.min, axis=AX.X), img)
                step_b(V.tensor_tensor(gtmp[:, n], gtmp[:, 2 + n], gred[:, 7 + 2 * n, :, 0:1].to_broadcast([TC, 2, 10]), op=ALU.is_equal), img)

            def gate(img, n):
                if n == 0:
                    dve.wait_ge(*read_out(img, "gl", 0))
                    V.tensor_reduce(gred[:, 0, :, 0], routed, op=ALU.max, axis=AX.X)
                    step_b(V.tensor_reduce(gred[:, 1], pairs(gsm), op=ALU.max, axis=AX.X), img)
                    V.tensor_tensor(glog[:, :, 0:10], routed, gred[:, 0, :, 0:1].to_broadcast([TC, 2, 10]), op=ALU.subtract)
                    V.tensor_tensor(pairs(glog), pairs(gsm), gred[:, 1].unsqueeze(3).to_broadcast([TC, 2, 2, 2]),
                                    op=ALU.subtract).then_inc(s_gmax.up(), 1)
                if n == 1:
                    dve.wait_ge(*s_gexp.at(img, 1))
                    V.tensor_reduce(gred[:, 2, :, 0], gexp[:, :, 0:10], op=ALU.add, axis=AX.X)
                    step_b(V.tensor_reduce(gred[:, 3], pairs(gexp), op=ALU.add, axis=AX.X), img)
                    V.reciprocal(gred[:, 4, :, 0], gred[:, 2, :, 0])
                    step_b(V.reciprocal(gred[:, 5], gred[:, 3]), img)
                    V.tensor_tensor(routed, gexp[:, :, 0:10], gred[:, 4, :, 0:1].to_broadcast([TC, 2, 10]), op=ALU.mult)
                    step_b(V.tensor_tensor(pairs(gsm), pairs(gexp), gred[:, 5].unsqueeze(3).to_broadcast([TC, 2, 2, 2]), op=ALU.mult), img)
                if n == 2:
                    first_best(img, routed, 0)
                    step_b(V.scalar_tensor_tensor(gtmp[:, 4], gtmp[:, 0], -4.0, routed, ALU.mult, ALU.add), img)
                    first_best(img, gtmp[:, 4], 1)
                if n == 3:
                    dve.wait_ge(*s_gn.at(img, 0))
                    step_b(V.tensor_tensor(gtmp[:, 5], gtmp[:, 0], gtmp[:, 1], op=ALU.add), img)
                    step_b(V.tensor_tensor(gtmp[:, 4], gtmp[:, 5], routed, op=ALU.mult), img)
                    step_b(V.tensor_reduce(gred[:, 10, :, 0], gtmp[:, 4], op=ALU.add, axis=AX.X), img)
                    step_b(V.tensor_scalar(gred[:, 10, :, 0], gred[:, 10, :, 0], GATE_EPS, None, ALU.max), img)
                    step_b(V.reciprocal(gred[:, 10, :, 1], gred[:, 10, :, 0]), img)
                    step_b(V.tensor_scalar(gred[:, 11], gsm[:, :, 12:14], 4.0, None, ALU.mult), img)
                    step_b(V.tensor_tensor(gred[:, 10, :, 0], gred[:, 10, :, 1], gred[:, 11, :, 1], op=ALU.mult), img)
                    by_chunk = mg[:].rearrange("p h c -> p c h")
                    V.tensor_tensor(by_chunk[:, :, 2:H], gtmp[:, 4], gred[:, 10, :, 0:1].to_broadcast([TC, 2, 10]), op=ALU.mult)
                    V.tensor_tensor(by_chunk[:, :, 0:2], gsm[:, :, 10:12], gred[:, 11, :, 0:1].to_broadcast([TC, 2, 2]),
                                    op=ALU.mult).then_inc(s_gate.up(), 1)

            def v2_(img, n):
                c, a = divmod(n, 2)
                dve.wait_ge(*made(img, "v2", n))
                V.tensor_scalar(v2[0:TC - c, c, 384 * a:384 * a + 384], psum("v2", n)[0:TC - c, 0:384], 1.0 / W_SCALE, None,
                                ALU.mult).then_inc(free("v2", n), 1)

            def var_(img, n):
                if n == 0:
                    dve.wait_ge(*made(img, "var", 0))
                    V.tensor_scalar(var[:], psum("var", 0)[:, 0:TP], LN_EPS, None, ALU.add).then_inc(free("var", 0), 1)
                    dve.wait_ge(*read_out(img, "var", 0))
                    step_b(V.tensor_scalar(rs[:].bitcast(I32), var[:].bitcast(I32), 1, None, ALU.logical_shift_right), img)
                    step_b(V.tensor_scalar(rs[:].bitcast(I32), rs[:].bitcast(I32), -1.0, RSQRT_GUESS, ALU.mult, ALU.add), img)
                elif n < 4:
                    step_b(V.tensor_tensor(newton[:], rs[:], rs[:], op=ALU.mult), img)
                    step_b(V.scalar_tensor_tensor(newton[:], newton[:], -0.5, var[:], ALU.mult, ALU.mult), img)
                    step_b(V.scalar_tensor_tensor(rs[:], newton[:], 1.5, rs[:], ALU.add, ALU.mult), img)
                else:
                    step_b(V.tensor_copy(rs_h[:], rs[:]), img)
                    V.tensor_tensor(rs_l[:], rs[:], rs_h[:], op=ALU.subtract).then_inc(s_rs.up(), 1)

            def low_parts(img, t):
                dve.wait_ge(*s_hi.at(img, t + 1))
                for j in range(2):
                    r = slice(64 * j, 64 * j + 64)
                    last = V.scalar_tensor_tensor(ql[r, 2 * t + j, :], qkn[r, t % QKN_SLOTS, 0, :], ln_b[r, 0:1], qh[r, 2 * t + j, :],
                                           ALU.add, ALU.subtract)
                last.then_inc(s_lo.up(), 1)

            def rstd_(img, t):
                dve.wait_ge(*made(img, "rstd", t))
                dve.wait_ge(*read_out(img, "qk", t))
                if t >= QKN_SLOTS:
                    dve.wait_ge(*s_kl.at(img, t + 1 - QKN_SLOTS))
                    dve.wait_ge(*s_lo.at(img, t + 1 - QKN_SLOTS))
                for s in range(2):
                    last = V.scalar_tensor_tensor(qkn[:, t % QKN_SLOTS, s, :], psum("rstd", t)[:, s * TP:s * TP + TP], ln_w[:, s:s + 1],
                                                  qkc[:, t, s, :], ALU.mult, ALU.mult)
                last.then_inc(free("rstd", t), 1)

            def s2(img, h):
                dve.wait_ge(*made(img, "s2", h))
                V.tensor_reduce(nmax2[:, h, :], psum("s2", h)[0:TC, 0:2 * T].rearrange("p (a b) -> p a b", a=2),
                                op=ALU.max, axis=AX.X, negate=True).then_inc(s_nm2.up(), 1)

            def gate_over_sum(img, t):
                heads = slice(2 * t, 2 * t + 2)
                for h in lasts("s2", (2 * t, 2 * t + 1)):
                    dve.wait_ge(*read_out(img, "s2", h))
                V.reciprocal(rsum2[:, heads, :], sum2[:, heads, :]).then_inc(s_rsum2.up(), 1)
                dve.wait_ge(*s_rsum2.at(img, t + 1))
                dve.wait_ge(*s_gate.at(img, 1))
                V.tensor_tensor(gn[:, heads, :], rsum2[:, heads, :], mg[:, heads, :], op=ALU.mult).then_inc(s_gn.up(), 1)

            def proj(img, _):
                dve.wait_ge(*made(img, "proj", 0))
                dve.wait_ge(*s_h2c.at(img, 1))
                dve.wait_ge(*s_out.at(img, 0))
                V.tensor_tensor(res[:].rearrange("p a b -> p (a b)"), psum("proj", 0)[0:TC, 0:2 * D],
                                h2c[:].rearrange("p a b -> p (a b)"), op=ALU.add).then_inc(free("proj", 0), 1)

            run_phases(dve, {"fold": fold, "tok": tok, "nx1": nx1, "nx2": nx2, "x1T": x1T_, "qk1": qk1_, "km": km, "s1": s1, "ctx": ctx_, "wo": wo, "x2T": x2T_, "gl": gl,
                             "gate": gate, "v2": v2_, "var": var_, "rstd": rstd_, "lo": low_parts, "s2": s2, "gr": gate_over_sum,
                             "proj": proj})

        for name, s in signals.items():
            times = {"x_loaded": 5, "stored": 5}.get(name, 4)
            assert s.made == times * s.per, (name, s.made, s.per)


def laid_out(x, L0_tok_freq_weight_h, L0_tok_freq_weight_w, L0_tok_proj_w, L0_tok_proj_b, L0_tok_cls_token,
             L0_tok_pos_emb, L0_attn_Wq, L0_attn_bq, L0_attn_Wk, L0_attn_bk, L0_attn_Wv, L0_attn_bv, L0_attn_Wo,
             L0_attn_bo, L0_ffn_qkv_w, L0_ffn_qkv_b, L0_ffn_q_norm_w, L0_ffn_q_norm_b, L0_ffn_k_norm_w,
             L0_ffn_k_norm_b, L0_ffn_wg_w, L0_ffn_wg0_w, L0_ffn_wg1_w, L0_ffn_proj_w, L0_ffn_proj_b):
    n = x.shape[0]
    first, mirror = fold_pairs()
    a = {}
    px = np.asarray(x).reshape(n, CH, SIDE, PATCH, SIDE, PATCH).transpose(0, 1, 3, 5, 2, 4).reshape(n, CH, PATCH * PATCH, NPATCH)
    for name, index in (("xa", first), ("xb", mirror)):
        rows = np.zeros((n, KC * KR, NPATCH), np.float32)
        rows[:, :CH * len(index)] = px[:, :, index].reshape(n, -1, NPATCH)
        a[name] = rows.reshape(n, KC, KR, NPATCH).transpose(0, 2, 1, 3)

    def chunked(row):
        return np.broadcast_to(np.asarray(row).reshape(-1), (TC, row.size))

    def kchunks(w, rows):
        w = np.asarray(w)
        return w.reshape(w.shape[0] // rows, rows, -1).transpose(1, 0, 2)

    a["proj_tok"] = np.asarray(L0_tok_proj_w).reshape(D, CH, 2, 72).transpose(3, 2, 1, 0)
    a["freq_h"] = np.repeat(L0_tok_freq_weight_h, PW).reshape(2, 72).T
    a["freq_w"] = np.tile(L0_tok_freq_weight_w, PATCH).reshape(2, 72).T
    pos = np.zeros((TP, D), np.float32)
    pos[:T] = L0_tok_pos_emb[0]
    add = np.zeros((TP, D), np.float32)
    add[0] = np.asarray(L0_tok_cls_token).reshape(-1)
    add[1:T] = L0_tok_proj_b
    a["pos"] = pos.reshape(2, TC, D).transpose(1, 0, 2)
    a["tok_add"] = add.reshape(2, TC, D).transpose(1, 0, 2)
    def biased(w, bias):
        w = np.asarray(w)
        rows = np.zeros((DB, 2, w.shape[1]), np.float32)
        rows[:DK] = kchunks(w, DK)
        rows[DK, 1] = bias
        return rows

    def by_head(w):
        return np.asarray(w).transpose(1, 0, 2).reshape(D, D)

    def twice(x):
        x = np.asarray(x).reshape(*x.shape[:-1], 3, 1, 64)
        return np.broadcast_to(x, (*x.shape[:-2], 2, 64)).reshape(*x.shape[:-3], 384)

    a["wqk1"] = biased(np.concatenate([twice(by_head(L0_attn_Wq)), twice(by_head(L0_attn_Wk))], axis=1),
                       np.concatenate([twice(np.asarray(L0_attn_bq).reshape(D)), twice(np.asarray(L0_attn_bk).reshape(D))]))
    a["wv1"] = biased(by_head(L0_attn_Wv), np.asarray(L0_attn_bv).reshape(D))
    wo = np.zeros((3, GROUP, 32, D), np.float32)
    wo[:, :, :E1] = np.asarray(L0_attn_Wo).reshape(3, GROUP, E1, D)
    a["wo1"] = wo.reshape(3, 128, D).transpose(1, 0, 2)
    a["bo1"] = chunked(L0_attn_bo)
    a["wgate"] = biased(np.concatenate([L0_ffn_wg_w, L0_ffn_wg1_w, L0_ffn_wg0_w], axis=1), 0.0)
    qkv, qkv_b = np.asarray(L0_ffn_qkv_w), np.asarray(L0_ffn_qkv_b)
    a["wqk"] = biased(qkv[:, :2 * H * E2], qkv_b[:2 * H * E2]).reshape(DB, 2, 2 * H, E2)
    a["wv2"] = biased(qkv[:, 2 * H * E2:], qkv_b[2 * H * E2:])
    a["ln_w"] = np.stack([np.tile(L0_ffn_q_norm_w, 2), np.tile(L0_ffn_k_norm_w, 2)], axis=1)
    a["ln_b"] = np.stack([np.tile(L0_ffn_q_norm_b, 2), np.tile(L0_ffn_k_norm_b, 2)], axis=1)
    a["wp2"] = kchunks(L0_ffn_proj_w, 128)
    a["bp2"] = chunked(L0_ffn_proj_b)
    a.update(shape_constants())
    return {k: np.ascontiguousarray(v) for k, v in a.items()}


def kernel(**inputs):
    import concourse.bacc as bacc
    from concourse.bass_utils import run_bass_kernel_spmd

    nc = bacc.Bacc("TRN2", target_bir_lowering=False, num_devices=1)
    arrays = laid_out(**inputs)
    images = inputs["x"].shape[0]
    ins = {k: nc.dram_tensor(f"in_{k}", v.shape, mybir.dt.from_np(v.dtype), kind="ExternalInput").ap() for k, v in arrays.items()}
    out = nc.dram_tensor("out_tokens", (images, T, D), F32, kind="ExternalOutput").ap()
    build_vit_block(nc, ins, out, images)
    r = run_bass_kernel_spmd(nc, [{f"in_{k}": v for k, v in arrays.items()}], core_ids=[0])
    return r.results[0]["out_tokens"]
```
